# Optimizing a Trainium2 kernel written in Bass

```python
import numpy as np
import jax
import jax.numpy as jnp

def _softmax(x, axis=-1):
    return jax.nn.softmax(x, axis=axis)

def _gelu(x):
    return jax.nn.gelu(x, approximate=True)

def _silu(x):
    return jax.nn.silu(x)

def _sigmoid(x):
    return jax.nn.sigmoid(x)

def _layernorm(x, axis=-1, eps=1e-05):
    m = jnp.mean(x, axis=axis, keepdims=True)
    v = jnp.var(x, axis=axis, keepdims=True)
    return (x - m) / jnp.sqrt(v + eps)

def _scatter_add(tgt, idx, src, axis=0):
    return tgt.at[idx].add(src)

def _segment_sum(src, seg, n):
    return jax.ops.segment_sum(src, seg, n)
kernel_name = 'mk_gnn_preln_d2_gnn_r8_07b3c5'

def setup_inputs(seed: int=0):
    np.random.seed(seed)
    _w = jnp.asarray

    def _rec_inputs():
        import jax
        import jax.numpy as jnp
        _gk = jax.random.key(seed)
        x = -0.000202 + 1 * jax.random.normal(jax.random.fold_in(_gk, 1), (12500, 64), jnp.float32)
        src = jax.random.randint(jax.random.fold_in(_gk, 2), (400000,), 0, 12500, jnp.int32)
        dst = jax.random.randint(jax.random.fold_in(_gk, 3), (400000,), 0, 12500, jnp.int32)
        _o = jnp.argsort(dst, stable=True)
        src = src[_o]
        dst = dst[_o]
        edge_attr_32 = jax.random.uniform(jax.random.fold_in(_gk, 12), (400000, 32), jnp.float32, 0.0, 1)
        edge_weight = jax.random.uniform(jax.random.fold_in(_gk, 14), (400000,), jnp.float32, 0.0, 1)
        return (x, src, dst, edge_attr_32, edge_weight)
    x, src, dst, edge_attr_32, edge_weight = _rec_inputs()

    def _L0_gnn_setup():
        import jax, jax.numpy as jnp
        import numpy as np
        N_NODES = 12500
        N_EDGES = 400000
        D_FEAT = 64
        K_HOPS = 3
        key = jax.random.key(seed)
        k1, k2, k3, k4 = jax.random.split(key, 4)
        x = jax.random.normal(k1, (N_NODES, D_FEAT), dtype=jnp.float32)
        edge_weight = jax.random.uniform(k2, (N_EDGES,), dtype=jnp.float32)
        src = jax.random.randint(k3, (N_EDGES,), 0, N_NODES, dtype=jnp.int32)
        dst = jax.random.randint(k4, (N_EDGES,), 0, N_NODES, dtype=jnp.int32)
        return {'x': x, 'edge_weight': edge_weight, 'src': src, 'dst': dst}
    _L0_gnn_all = _L0_gnn_setup()
    _L0_gnn_in = {k: v for k, v in _L0_gnn_all.items() if k in ()}
    del _L0_gnn_all

    def _L1_gnn_setup():
        import jax, jax.numpy as jnp
        import numpy as np
        N_NODES = 6250
        N_EDGES = 100000
        C = 64
        EDGE_DIM = 32
        Z_DIM = 2 * C + EDGE_DIM
        key = jax.random.key(seed)
        ks = jax.random.split(key, 10)
        s = 1.0 / np.sqrt(Z_DIM)
        sm = 1.0 / np.sqrt(C)
        return {'x': jax.random.normal(ks[0], (N_NODES, C), dtype=jnp.float32), 'edge_attr': jax.random.uniform(ks[1], (N_EDGES, EDGE_DIM), dtype=jnp.float32), 'Wf': jax.random.uniform(ks[2], (Z_DIM, C), minval=-s, maxval=s, dtype=jnp.float32), 'bf': jax.random.uniform(ks[3], (C,), minval=-s, maxval=s, dtype=jnp.float32), 'Ws': jax.random.uniform(ks[4], (Z_DIM, C), minval=-s, maxval=s, dtype=jnp.float32), 'bs': jax.random.uniform(ks[5], (C,), minval=-s, maxval=s, dtype=jnp.float32), 'Wm': jax.random.uniform(ks[6], (C, C), minval=-sm, maxval=sm, dtype=jnp.float32), 'bm': jax.random.uniform(ks[7], (C,), minval=-sm, maxval=sm, dtype=jnp.float32), 'edge_index': jax.random.randint(ks[8], (2, N_EDGES), 0, N_NODES, dtype=jnp.int64) if jax.config.jax_enable_x64 else jax.random.randint(ks[8], (2, N_EDGES), 0, N_NODES, dtype=jnp.int32)}
    _L1_gnn_all = _L1_gnn_setup()
    _L1_gnn_in = {k: v for k, v in _L1_gnn_all.items() if k in ('Wf', 'bf', 'Ws', 'bs', 'Wm', 'bm')}
    del _L1_gnn_all
    return {'x': x, 'src': src, 'dst': dst, 'edge_attr_32': edge_attr_32, 'edge_weight': edge_weight, 'L1_gnn_Wf': _L1_gnn_in['Wf'], 'L1_gnn_bf': _L1_gnn_in['bf'], 'L1_gnn_Ws': _L1_gnn_in['Ws'], 'L1_gnn_bs': _L1_gnn_in['bs'], 'L1_gnn_Wm': _L1_gnn_in['Wm'], 'L1_gnn_bm': _L1_gnn_in['bm']}

def reference(x, src, dst, edge_attr_32, edge_weight, L1_gnn_Wf, L1_gnn_bf, L1_gnn_Ws, L1_gnn_bs, L1_gnn_Wm, L1_gnn_bm):
    import jax
    import jax.numpy as jnp

    def _L0_gnn_ref(x, edge_weight, src, dst):
        import jax, jax.numpy as jnp
        import numpy as np
        N_NODES = 12500
        N_EDGES = 400000
        D_FEAT = 64
        K_HOPS = 3
        h = x
        for _ in range(K_HOPS):
            msg = h[src] * edge_weight[:, None]
            h = jax.ops.segment_sum(msg, dst, num_segments=N_NODES)
        return h

    def _L1_gnn_ref(x, edge_attr, Wf, bf, Ws, bs, Wm, bm, edge_index):
        import jax, jax.numpy as jnp
        import numpy as np
        N_NODES = 6250
        N_EDGES = 100000
        C = 64
        EDGE_DIM = 32
        Z_DIM = 2 * C + EDGE_DIM
        src = edge_index[0]
        dst = edge_index[1]
        z = jnp.concatenate([x[dst], x[src], edge_attr], axis=-1)
        msg = jax.nn.sigmoid(z @ Wf + bf) * jax.nn.softplus(z @ Ws + bs)
        agg = jax.ops.segment_sum(msg, dst, num_segments=x.shape[0])
        h = agg + x
        return jax.nn.relu(h @ Wm + bm)
    edge_index = jnp.stack([src, dst])
    h = jnp.maximum(_layernorm(x, axis=-1), 0.0)
    x = x + _L0_gnn_ref(h, edge_weight, src, dst)
    h = jnp.maximum(_layernorm(x, axis=-1), 0.0)
    x = x + _L1_gnn_ref(h, edge_attr_32, L1_gnn_Wf, L1_gnn_bf, L1_gnn_Ws, L1_gnn_bs, L1_gnn_Wm, L1_gnn_bm, edge_index)
    return x

_drawn_inputs = setup_inputs


def setup_inputs(seed=0):
    import zlib

    import numpy as np

    out = dict(_drawn_inputs(seed))
    spreads = {}
    factors = {'x': 2.999,
     'edge_attr_32': 8.0,
     'L1_gnn_Wf': 8.0,
     'L1_gnn_bf': 54.468,
     'L1_gnn_Ws': 8.0,
     'L1_gnn_bs': 46.254,
     'L1_gnn_Wm': 8.0,
     'L1_gnn_bm': 64.0}
    for name, (base, spread) in spreads.items():
        noise = np.random.default_rng([zlib.crc32(name.encode()), seed]).standard_normal(out[name].shape)
        drawn = base * np.exp(spread * noise) if base else spread * noise
        out[name] = jnp.asarray(drawn.astype(out[name].dtype))
    for name, factor in factors.items():
        out[name] = (out[name] * factor).astype(out[name].dtype)
    return out
```

```python
from contextlib import ExitStack

import concourse.bass as bass
from concourse import mybir

P = 128
F32 = mybir.dt.float32
I32 = mybir.dt.int32
ALU = mybir.AluOpType
ACT = mybir.ActivationFunctionType
AX = mybir.AxisListType
DVE_ENGINE = mybir.EngineType.DVE
SP_ENGINE = mybir.EngineType.SP

HOPS = 3
GROUP = 5
GROUPS_IN_BODY = 5
BATCH = 7
EPS = 1e-5


def build(nc, x, src_t, dst_t, dst_rows, w_t, attr_t, w_f, w_s, b_f, b_s, w_m, b_m, out):
    NODES, FEAT = x.shape
    TILES = src_t.shape[1]
    EDIM = attr_t.shape[0]
    BODY = GROUP * GROUPS_IN_BODY
    ROUNDS = TILES // BODY
    GROUPS = TILES // GROUP
    NT = -(-NODES // P)
    NT_FULL = NODES // P
    NREST = NODES - NT_FULL * P
    NBATCH = NT // BATCH
    RT = -(-(NODES + P) // (P * BATCH)) * BATCH
    RBATCH = RT // BATCH
    RANKS = RT * P
    F2 = 2 * FEAT
    HALVES = [(0, NT // 2), (NT // 2, NT)]
    chunks = [(a, min(a + 512, TILES)) for a in range(0, TILES, 512)]
    assert dst_t.shape[0] == P and TILES % BODY == 0 and NT % BATCH == 0 and FEAT == 64

    CREDIT = BODY

    SLOT3 = (0, 1, 0, 1, 2)
    FILLS = (2, 2, 1)
    FILL_NO = (0, 0, 1, 1, 0)

    ctx = ExitStack()
    with ctx:
        def sb(name, shape, dt=F32):
            return ctx.enter_context(nc.sbuf_tensor(name, shape, dt))

        def sem(name):
            return ctx.enter_context(nc.semaphore(name))

        def dram(name, shape, dt=F32):
            return nc.dram_tensor(name, shape, dt, kind="Internal").ap()

        h_table = dram("h_table", (NT * P, FEAT))
        src_table = dram("src_table", (NT * P, F2))
        dst_by_rank = dram("dst_by_rank", (RANKS, F2))
        base_dram = dram("base_dram", (TILES, 1))
        first_rank_dram = dram("first_rank_dram", (NT, 1), I32)
        node_dram = dram("node_dram", (RANKS, 1))

        acc = sb("acc", [P, RANKS])
        xs = sb("xs", [P, NT, FEAT])
        h = sb("h", [P, NT, FEAT])
        src = sb("src", [P, TILES + BODY], I32)
        w = sb("w", [P, TILES])
        rel = sb("rel", [P, TILES])
        first_dst = sb("first_dst", [P, TILES])
        gathered = sb("gathered", [P, BODY, F2])
        idx = sb("idx", [P, BODY], I32)
        msg = sb("msg", [P, GROUP, FEAT + 1])
        pick = sb("pick", [P, 3, GROUP, P])
        iota = sb("iota", [P, P])
        part = sb("part", [P, 4])
        nbase = sb("nbase", [P, NT])
        ident = sb("ident", [P, P])
        tri = sb("tri", [P, P])
        stats = sb("stats", [P, 4, NT])
        eps = sb("eps", [P, 1])
        small = sb("small", [P, 8])
        small_i = sb("small_i", [P, 2], I32)
        node_f = sb("node_f", [P, RT])
        node_i = sb("node_i", [P, RT], I32)
        node_idx = sb("node_idx", [P, BATCH], I32)
        w_src = sb("w_src", [FEAT, F2])
        w_dst = sb("w_dst", [FEAT + 1, F2])
        w_edge = sb("w_edge", [EDIM, F2])
        w_out = sb("w_out", [FEAT + 1, FEAT])

        scratch = sb("scratch", [P, 4 * BATCH * P])
        in_batch = scratch[:, :].rearrange("p (n m c) -> p n m c", n=4, m=BATCH)
        stage, turned, spread, rows_out = (in_batch[:, n] for n in range(4))
        G1 = GROUP * P
        in_group = scratch[:, 0:4 * G1].rearrange("p (n j c) -> p n j c", n=4, j=GROUP)
        pick_t, z, e, lg = (in_group[:, n] for n in range(4))
        iota_i = scratch[:, 0:P].bitcast(I32)
        nbase_i = scratch[:, P:P + NT].bitcast(I32)
        part_i = scratch[:, 2 * P:2 * P + 1].bitcast(I32)
        q_win = sb("q_win", [P, 3, GROUP, F2])
        attr = sb("attr", [EDIM, 3, GROUP * P])

        psum = ctx.enter_context(nc.psum_tensor("psum", [P, 8 * 512], F32))
        ps_sum = psum[:, 0:G1].rearrange("p (j c) -> p j c", j=GROUP)
        ps_turn = psum[:, 1024:1024 + G1].rearrange("p (j c) -> p j c", j=GROUP)
        ps_z = psum[:, 2048:2048 + G1].rearrange("p (j c) -> p j c", j=GROUP)
        ps_a = psum[:, 0:BATCH * P].rearrange("p (m c) -> p m c", m=BATCH)
        ps_b = psum[:, 1024:1024 + BATCH * P].rearrange("p (m c) -> p m c", m=BATCH)

        dst_now = acc[:, 0:TILES].bitcast(I32)
        dst_before = acc[:, TILES:2 * TILES].bitcast(I32)
        is_first = acc[:, 2 * TILES:3 * TILES]
        last_dst = acc[0:NT, 3 * TILES:4 * TILES].bitcast(I32)
        ROW = 96
        steps_row = acc[ROW:ROW + 1, 0:TILES]
        ones_row = acc[ROW:ROW + 1, TILES:2 * TILES]
        base_row = acc[ROW:ROW + 1, 2 * TILES:3 * TILES]
        base_regs = acc[ROW:ROW + 1, 0:8 * GROUPS].bitcast(I32)
        first_rank_regs = acc[ROW:ROW + 1, 8 * GROUPS:8 * GROUPS + 8 * NBATCH].bitcast(I32)
        dst_at = scratch[0:NT, 0:P].bitcast(I32)
        below = scratch[0:NT, P:2 * P]
        differs = scratch[0:NT, 2 * P:3 * P]
        is_last_below = acc[0:NT, 2 * TILES:3 * TILES]

        pool_passed = sem("pool_passed")
        pe_passed = sem("pe_passed")
        dve_passed = sem("dve_passed")
        consts_made = sem("consts_made")
        x_loaded = sem("x_loaded")
        dst_loaded = sem("dst_loaded")
        dst_shifted = sem("dst_shifted")
        before_set = sem("before_set")
        last_loaded = sem("last_loaded")
        src_loaded = sem("src_loaded")
        w_loaded = sem("w_loaded")
        weights_loaded = sem("weights_loaded")
        dve_chain = sem("dve_chain")
        tail_zeroed = sem("tail_zeroed")
        var_ready = sem("var_ready")
        std_ready = sem("std_ready")
        h_ready = sem("h_ready")
        table_ready = sem("table_ready")
        tri_ready = sem("tri_ready")
        flags_ready = sem("flags_ready")
        rel_turned = sem("rel_turned")
        rel_copied = sem("rel_copied")
        steps_ready = sem("steps_ready")
        base_ready = sem("base_ready")
        base_stored = sem("base_stored")
        at_ready = sem("at_ready")
        at_gathered = sem("at_gathered")
        first_ready = sem("first_ready")
        first_stored = sem("first_stored")
        first_loaded = sem("first_loaded")
        regs_ready = sem("regs_ready")
        idx_ready = sem("idx_ready")
        gather_done = [sem(f"gather_done_{j}") for j in range(BODY)]
        slot_free = sem("slot_free")
        pick_ready = sem("pick_ready")
        sums_ready = sem("sums_ready")
        sums_added = sem("sums_added")
        staged = sem("staged")
        acc_zero = sem("acc_zero")
        turn_done = sem("turn_done")
        turn_copied = sem("turn_copied")
        spread_ready = sem("spread_ready")
        batch_done = sem("batch_done")
        batch_kept = sem("batch_kept")
        residual_done = sem("residual_done")
        node_stored = sem("node_stored")
        node_loaded = sem("node_loaded")
        node_idx_ready = sem("node_idx_ready")
        node_rows = [sem(f"node_rows_{m}") for m in range(BATCH)]
        node_used = sem("node_used")
        p_staged = sem("p_staged")
        p_turned = sem("p_turned")
        p_copied = sem("p_copied")
        p_done = sem("p_done")
        p_kept = sem("p_kept")
        p_stored = sem("p_stored")
        group_loaded = [sem(f"group_loaded_{s}") for s in range(3)]
        pick_turned = sem("pick_turned")
        pick_t_ready = sem("pick_t_ready")
        z_done = sem("z_done")
        z_ready = sem("z_ready")
        z_read = sem("z_read")
        gate_arg = sem("gate_arg")
        soft_ready = sem("soft_ready")
        logs_ready = sem("logs_ready")
        act_steps = sem("act_steps")
        gate_ready = sem("gate_ready")
        msg_ready = sem("msg_ready")
        conv_sums = sem("conv_sums")
        conv_added = sem("conv_added")
        f_kept = sem("f_kept")
        out_stored = sem("out_stored")

        h_table_v = h_table.rearrange("(k p) f -> p k f", p=P)
        src_table_v = src_table.rearrange("(k p) f -> p k f", p=P)
        rank_v = dst_by_rank.rearrange("(p j) f -> p j f", p=P)

        block = ctx.enter_context(nc.Block())

        @block.sync
        def _(sp):
            sp.wait_ge(tail_zeroed, 1)
            sp.dma_start(xs[:, 0:NT_FULL, :], x[0:NT_FULL * P].rearrange("(k p) f -> p k f", p=P)).then_inc(x_loaded, 16)
            sp.dma_start(xs[0:NREST, NT_FULL, :], x[NT_FULL * P:NODES]).then_inc(x_loaded, 16)
            sp.dma_start(src[:, 0:TILES], src_t).then_inc(src_loaded, 16)
            sp.dma_start(src[:, TILES:TILES + BODY], src_t[:, 0:BODY]).then_inc(src_loaded, 16)
            sp.dma_start(w[:, :], w_t).then_inc(w_loaded, 16)
            for dst_ap, a in ((w_dst[0:FEAT], (0, FEAT)), (w_src[:], (FEAT, F2)), (w_edge[:], (F2, F2 + EDIM))):
                sp.dma_start(dst_ap[:, 0:FEAT], w_f[a[0]:a[1]]).then_inc(weights_loaded, 16)
                sp.dma_start(dst_ap[:, FEAT:F2], w_s[a[0]:a[1]]).then_inc(weights_loaded, 16)
            sp.dma_start(w_dst[FEAT:FEAT + 1, 0:FEAT], b_f).then_inc(weights_loaded, 16)
            sp.dma_start(w_dst[FEAT:FEAT + 1, FEAT:F2], b_s).then_inc(weights_loaded, 16)
            sp.dma_start(w_out[0:FEAT, :], w_m).then_inc(weights_loaded, 16)
            sp.dma_start(w_out[FEAT:FEAT + 1, :], b_m).then_inc(weights_loaded, 16)

            for n, (a, z1) in enumerate(HALVES):
                sp.wait_ge(h_ready, n + 1)
                sp.dma_start(h_table_v[:, a:z1, :], h[:, a:z1, :]).then_inc(table_ready, 8 * NBATCH)

            sp.wait_ge(base_ready, 1)
            sp.dma_start(base_dram.rearrange("t o -> o t"), base_row).then_inc(base_stored, 16)
            sp.wait_ge(first_ready, 1)
            sp.dma_start(first_rank_dram, small_i[0:NT, 1:2]).then_inc(first_stored, 16)
            sp.wait_ge(first_stored, 16)
            sp.wait_ge(regs_ready, 1)
            sp.dma_start(first_rank_regs.rearrange("o (b e) -> o b e", e=8)[:, :, 0:BATCH],
                         first_rank_dram.rearrange("(b e) o -> o b e", e=BATCH)).then_inc(first_loaded, 16)

            with sp.Fori(0, HOPS) as hop:
                with sp.Fori(0, NBATCH) as b:
                    sp.wait_ge(batch_kept, hop * NBATCH + b + 1)
                    sp.dma_start(h_table_v[:, bass.ds(b * BATCH, BATCH), :],
                                 h[:, bass.ds(b * BATCH, BATCH), :]).then_inc(table_ready, 16)

            sp.wait_ge(batch_kept, HOPS * NBATCH)
            sp.dma_start(node_dram.rearrange("r o -> o r"), acc[FEAT:FEAT + 1, :]).then_inc(node_stored, 16)
            sp.wait_ge(node_stored, 16)
            sp.dma_start(node_f[:, :], node_dram.rearrange("(p j) o -> p (j o)", p=P)).then_inc(node_loaded, 16)
            sp.wait_ge(table_ready, 16 * NBATCH * (HOPS + 1))
            for n, (a, z1) in enumerate(HALVES):
                sp.wait_ge(h_ready, n + 3)
                sp.dma_start(h_table_v[:, a:z1, :], h[:, a:z1, :]).then_inc(table_ready, 8 * NBATCH)
            with sp.Fori(0, NBATCH) as b:
                sp.wait_ge(p_kept, CREDIT + b + 1)
                sp.dma_start(src_table_v[:, bass.ds(b * BATCH, BATCH), :], rows_out).then_inc(p_stored, 16)
            with sp.Fori(0, RBATCH) as b:
                sp.wait_ge(p_kept, b + (CREDIT + NBATCH + 1))
                sp.dma_start(rank_v[:, bass.ds(b * BATCH, BATCH), :], rows_out).then_inc(p_stored, 16)
            sp.wait_ge(p_stored, CREDIT * 16 + 16 * (NBATCH + RBATCH))

            def load_group(i, q):
                s = SLOT3[q]
                g = i * GROUPS_IN_BODY + q
                _, ranks = nc.values_load_multi_w_load_instructions(
                    base_regs[:, bass.ds(g * 8, GROUP)], engines=[SP_ENGINE], min_val=0, max_val=RANKS - P,
                    skip_runtime_bounds_check_because="ranks are below the number of nodes")
                sp.wait_ge(z_done, g + (CREDIT - 1))
                sp.dma_start(attr[:, s, :], attr_t[:, bass.ds(g * (GROUP * P), GROUP * P)]).then_inc(group_loaded[s], 16)
                for j in range(GROUP):
                    sp.dma_start(q_win[:, s, j, :], dst_by_rank[bass.ds(ranks[j], P), :]).then_inc(group_loaded[s], 16)

            with sp.Fori(0, ROUNDS) as i:
                for q in range(GROUPS_IN_BODY):
                    load_group(i, q)

            with sp.Fori(0, NBATCH - 1) as b:
                sp.wait_ge(f_kept, b + (CREDIT + 1))
                sp.dma_start(out[bass.ds(b * (BATCH * P), BATCH * P), :].rearrange("(k p) f -> p k f", p=P),
                             rows_out[:, :, 0:FEAT]).then_inc(out_stored, 16)
            sp.wait_ge(f_kept, CREDIT + NBATCH)
            last = (NBATCH - 1) * BATCH * P
            sp.dma_start(out[last:NT_FULL * P, :].rearrange("(k p) f -> p k f", p=P),
                         rows_out[:, 0:BATCH - 1, 0:FEAT]).then_inc(out_stored, 16)
            sp.dma_start(out[NT_FULL * P:NODES, :], rows_out[0:NREST, BATCH - 1, 0:FEAT]).then_inc(out_stored, 16)
            sp.wait_ge(out_stored, 16 * (CREDIT + NBATCH + 1))

        @block.gpsimd
        def _(pool):
            nc.gpsimd.iota(iota_i[:, :], pattern=[[1, P]], base=0, channel_multiplier=0).then_inc(consts_made, 1)
            nc.gpsimd.iota(part_i[:, :], pattern=[[0, 1]], base=0, channel_multiplier=1).then_inc(consts_made, 1)
            nc.gpsimd.iota(nbase_i[:, :], pattern=[[P, NT]], base=0, channel_multiplier=0).then_inc(consts_made, 1)

            def gather(out_ap, table, index, done):
                pool.indirect_dma_start(out=out_ap, out_offset=None, in_=table,
                                        in_offset=bass.IndirectOffsetOnAxis(ap=index, axis=0)).then_inc(done, 16)

            pool.wait_ge(at_ready, 1)
            pool.wait_ge(base_stored, 16)
            gather(dst_at, dst_rows, small_i[0:NT, 0:1], at_gathered)
            gather(small[0:NT, 0:1], base_dram, small_i[0:NT, 0:1], at_gathered)

            def gather_group(phase, i, q, table, width):
                g = (phase * ROUNDS + i) * GROUPS_IN_BODY + q
                pool.wait_ge(idx_ready, g + 1)
                pool.wait_ge(slot_free, g * GROUP + GROUP)
                pool.sem_inc(pool_passed, 1)
                for j in range(GROUP):
                    k = q * GROUP + j
                    gather(gathered[:, k, 0:width], table, idx[:, k:k + 1], gather_done[k])

            with pool.Fori(0, HOPS) as hop:
                pool.wait_ge(table_ready, (hop + 1) * (16 * NBATCH))
                pool.sem_inc(pool_passed, 1)
                with pool.Fori(0, ROUNDS) as i:
                    for q in range(GROUPS_IN_BODY):
                        gather_group(hop, i, q, h_table, FEAT)

            pool.wait_ge(table_ready, 16 * NBATCH * (HOPS + 2))
            with pool.Fori(0, RBATCH) as b:
                pool.wait_ge(node_idx_ready, b + 1)
                pool.wait_ge(node_used, b + CREDIT)
                pool.sem_inc(pool_passed, 1)
                for m in range(BATCH):
                    gather(gathered[:, m, 0:FEAT], h_table, node_idx[:, m:m + 1], node_rows[m])

            pool.wait_ge(p_stored, 16 * (CREDIT + NBATCH))
            pool.wait_ge(node_used, RBATCH + CREDIT)
            with pool.Fori(0, ROUNDS) as i:
                for q in range(GROUPS_IN_BODY):
                    gather_group(HOPS, i, q, src_table, F2)

        @block.scalar
        def _(act):
            act.sem_inc(slot_free, CREDIT)
            act.sem_inc(p_stored, 16 * CREDIT)
            act.sem_inc(out_stored, 16 * CREDIT)
            act.dma_start(dst_now, dst_t).then_inc(dst_loaded, 16)
            act.dma_start(dst_before[1:P, :], dst_t[0:P - 1, :]).then_inc(dst_loaded, 16)
            act.dma_start(dst_before[0:1, 1:TILES], dst_t[P - 1:P, 0:TILES - 1]).then_inc(dst_loaded, 16)
            act.dma_start(last_dst, dst_t[P - 1:P, :].to_broadcast([NT, TILES])).then_inc(last_loaded, 16)

            def std(n):
                a, z1 = HALVES[(n - 1) % 2]
                act.wait_ge(var_ready, n)
                nc.scalar.activation(stats[:, 2, a:z1], stats[:, 1, a:z1], ACT.Sqrt, bias=eps[:, :],
                                     scale=1.0 / FEAT).then_inc(std_ready, 1)

            std(1)
            std(2)
            for n, (a, z1) in enumerate(chunks):
                act.wait_ge(rel_turned, n + 1)
                nc.scalar.copy(rel[:, a:z1], psum[:, n * 512:n * 512 + z1 - a]).then_inc(rel_copied, 1)
            act.wait_ge(flags_ready, 2)
            for n, (a, z1) in enumerate(chunks):
                act.wait_ge(rel_turned, len(chunks) + n + 1)
                nc.scalar.copy(steps_row[:, a:z1], psum[0:1, n * 512:n * 512 + z1 - a]).then_inc(steps_ready, 1)

            def scale_group(phase, i, q):
                r = phase * ROUNDS + i
                g = r * GROUPS_IN_BODY + q
                t = i * BODY + q * GROUP
                act.wait_ge(sums_ready, g * GROUP + CREDIT)
                nc.scalar.copy(msg[:, :, FEAT], first_dst[:, bass.ds(t, GROUP)])
                for j in range(GROUP):
                    k = q * GROUP + j
                    act.wait_ge(gather_done[k], r * 16 + 16)
                    nc.scalar.activation(msg[:, j, 0:FEAT], gathered[:, k, 0:FEAT], ACT.Copy,
                                         scale=w[:, bass.ds(t + j, 1)]).then_inc(slot_free, 1)

            def copy_turned(n):
                act.wait_ge(turn_done, n + 1)
                nc.scalar.copy(turned[:, :, 0:FEAT + 1], ps_a[:, :, 0:FEAT + 1]).then_inc(turn_copied, 1)

            act.wait_ge(w_loaded, 16)
            act.wait_ge(flags_ready, 2)
            with act.Fori(0, HOPS) as hop:
                with act.Fori(0, ROUNDS) as i:
                    for q in range(GROUPS_IN_BODY):
                        scale_group(hop, i, q)
                with act.Fori(0, NBATCH) as b:
                    n = hop * NBATCH + b
                    copy_turned(n)
                    act.wait_ge(batch_done, n + 1)
                    nc.scalar.copy(h[:, bass.ds(b * BATCH, BATCH), :], ps_b[:, :, 0:FEAT]).then_inc(batch_kept, 1)

            std(3)
            std(4)

            def copy_project(n, width):
                act.wait_ge(p_turned, n + (CREDIT + 1))
                nc.scalar.copy(turned[0:FEAT, :, :], ps_a[0:FEAT, :, :]).then_inc(p_copied, 1)

            act.wait_ge(h_ready, 4)
            with act.Fori(0, NBATCH) as b:
                act.wait_ge(p_turned, b + CREDIT)
                nc.scalar.copy(stage[:, :, 0:FEAT], h[:, bass.ds(b * BATCH, BATCH), :]).then_inc(p_staged, 1)
                copy_project(b, F2)
            with act.Fori(0, RBATCH) as b:
                copy_project(b + NBATCH, F2)

            def turn_pick(g):
                act.wait_ge(pick_turned, g + 1)
                nc.scalar.copy(pick_t, ps_turn).then_inc(pick_t_ready, 1)

            def gate_of(g):
                act.wait_ge(gate_arg, g + 1)
                nc.scalar.activation(lg[:, :, 0:FEAT], lg[:, :, 0:FEAT], ACT.Exp).then_inc(gate_ready, 1)

            def log_terms(g):
                act.wait_ge(z_ready, g + 1)
                nc.scalar.activation(e, z, ACT.Abs).then_inc(act_steps, 1)
                act.wait_ge(act_steps, g * 2 + 1)
                nc.scalar.activation(e, e, ACT.Exp, scale=-1.0).then_inc(act_steps, 1)
                act.wait_ge(act_steps, g * 2 + 2)
                act.wait_ge(msg_ready, g + CREDIT)
                nc.scalar.activation(lg, e, ACT.Ln, bias=1.0).then_inc(logs_ready, 1)

            turn_pick(0)
            log_terms(0)
            with act.Fori(0, GROUPS - 1) as g:
                turn_pick(g + 1)
                gate_of(g)
                log_terms(g + 1)
            gate_of(GROUPS - 1)

            with act.Fori(0, NBATCH) as b:
                copy_turned(b + HOPS * NBATCH)
            act.wait_ge(residual_done, 2)
            with act.Fori(0, NBATCH) as b:
                n = b + (NBATCH + RBATCH)
                act.wait_ge(p_turned, n + CREDIT)
                nc.scalar.copy(stage[:, :, 0:FEAT], h[:, bass.ds(b * BATCH, BATCH), :]).then_inc(p_staged, 1)
                copy_project(n, FEAT)

        @block.tensor
        def _(pe):
            pe.sem_inc(sums_ready, CREDIT)
            pe.sem_inc(p_turned, CREDIT)
            pe.sem_inc(z_done, CREDIT)
            pe.sem_inc(node_used, CREDIT)
            pe.wait_ge(tri_ready, 1)
            pe.wait_ge(flags_ready, 1)
            for n, (a, z1) in enumerate(chunks):
                pe.matmul(psum[:, n * 512:n * 512 + z1 - a], tri[:, :], is_first[:, a:z1],
                          start=True, stop=True).then_inc(rel_turned, 1)
            for n, (a, z1) in enumerate(chunks):
                pe.wait_ge(rel_copied, n + 1)
                if a == 0:
                    pe.matmul(psum[0:1, 0:1], ident[:, 0:1], is_first[:, 0:1], start=True, stop=True)
                    pe.matmul(psum[0:1, 1:z1], ident[:, 0:1], is_first[:, 1:z1], start=True, stop=False)
                    pe.matmul(psum[0:1, 1:z1], tri[:, P - 1:P], is_first[:, 0:z1 - 1],
                              start=False, stop=True).then_inc(rel_turned, 1)
                else:
                    to = psum[0:1, n * 512:n * 512 + z1 - a]
                    pe.matmul(to, ident[:, 0:1], is_first[:, a:z1], start=True, stop=False)
                    pe.matmul(to, tri[:, P - 1:P], is_first[:, a - 1:z1 - 1],
                              start=False, stop=True).then_inc(rel_turned, 1)

            pe.wait_ge(steps_ready, len(chunks))

            def sum_group(phase, i, q):
                n0 = ((phase * ROUNDS + i) * GROUPS_IN_BODY + q) * GROUP
                pe.wait_ge(sums_added, n0 + CREDIT)
                for j in range(GROUP):
                    pe.wait_ge(slot_free, n0 + (CREDIT + j + 1))
                    pe.wait_ge(pick_ready, n0 + (j + 1))
                    pe.matmul(ps_sum[0:FEAT + 1, j, :], msg[:, j, :], pick[:, 0, j, :],
                              start=True, stop=True).then_inc(sums_ready, 1)

            def turn_batch(n):
                pe.wait_ge(staged, n + 1)
                for m in range(BATCH):
                    mm = pe.transpose(ps_a[:, m, 0:FEAT + 1], stage[0:FEAT + 1, m, :], ident[0:FEAT + 1, 0:FEAT + 1])
                mm.then_inc(turn_done, 1)

            def spread_batch(n):
                pe.wait_ge(spread_ready, n + 1)
                for m in range(BATCH):
                    mm = pe.matmul(ps_b[:, m, 0:FEAT], spread[:, m, :], turned[:, m, 0:FEAT], start=True, stop=True)
                mm.then_inc(batch_done, 1)

            with pe.Fori(0, HOPS) as hop:
                with pe.Fori(0, ROUNDS) as i:
                    for q in range(GROUPS_IN_BODY):
                        sum_group(hop, i, q)
                with pe.Fori(0, NBATCH) as b:
                    n = hop * NBATCH + b
                    turn_batch(n)
                    spread_batch(n)

            def project(n, rows, weights, k, width):
                for m in range(BATCH):
                    mm = pe.transpose(ps_a[0:FEAT, m, :], rows(m), ident[:, :])
                mm.then_inc(p_turned, 1)
                pe.wait_ge(p_copied, n + 1)
                pe.wait_ge(p_kept, n + CREDIT)
                for m in range(BATCH):
                    mm = pe.matmul(ps_b[:, m, 0:width], turned[0:k, m, :], weights, start=True, stop=True)
                mm.then_inc(p_done, 1)

            pe.wait_ge(weights_loaded, 16 * 10)
            pe.wait_ge(residual_done, 1)
            with pe.Fori(0, NBATCH) as b:
                pe.wait_ge(p_staged, b + 1)
                pe.sem_inc(pe_passed, 1)
                project(b, lambda m: stage[:, m, 0:FEAT], w_src[:, :], FEAT, F2)
            with pe.Fori(0, RBATCH) as b:
                for m in range(BATCH):
                    pe.wait_ge(node_rows[m], b * 16 + 16)
                pe.sem_inc(pe_passed, 1)
                n = b + NBATCH
                for m in range(BATCH):
                    mm = pe.transpose(ps_a[0:FEAT, m, :], gathered[:, m, 0:FEAT], ident[:, :])
                mm.then_inc(p_turned, 1)
                pe.wait_ge(p_copied, n + 1)
                pe.sem_inc(node_used, 1)
                pe.wait_ge(p_kept, n + CREDIT)
                for m in range(BATCH):
                    mm = pe.matmul(ps_b[:, m, :], turned[0:FEAT + 1, m, :], w_dst[:, :], start=True, stop=True)
                mm.then_inc(p_done, 1)
            pe.wait_ge(p_kept, CREDIT + NBATCH + RBATCH)

            PHASE0 = HOPS * TILES

            def turn_picks(g, q):
                s = SLOT3[q]
                pe.wait_ge(pick_ready, g * GROUP + (PHASE0 + GROUP))
                for j in range(GROUP):
                    mm = pe.transpose(ps_turn[:, j, :], pick[:, s, j, :], ident[:, :])
                mm.then_inc(pick_turned, 1)

            def edge_products(i, g, q):
                s = SLOT3[q]
                pe.wait_ge(pick_t_ready, g + 1)
                pe.wait_ge(group_loaded[s], (i * FILLS[s] + FILL_NO[q] + 1) * (16 * (GROUP + 1)))
                pe.wait_ge(z_read, g + CREDIT)
                for j in range(GROUP):
                    pe.matmul(ps_z[:, j, :], pick_t[:, j, :], q_win[:, s, j, :], start=True, stop=False)
                    mm = pe.matmul(ps_z[:, j, :], attr[:, s, j * P:(j + 1) * P], w_edge[:, :], start=False, stop=True)
                mm.then_inc(z_done, 1)

            def sum_messages(g, q):
                s = SLOT3[q]
                pe.wait_ge(msg_ready, g + (CREDIT + 1))
                pe.wait_ge(sums_added, g * GROUP + (PHASE0 + CREDIT))
                for j in range(GROUP):
                    pe.matmul(ps_sum[0:FEAT, j, :], msg[:, j, 0:FEAT], pick[:, s, j, :],
                              start=True, stop=True).then_inc(sums_ready, 1)

            turn_picks(0, 0)
            edge_products(0, 0, 0)
            with pe.Fori(0, ROUNDS - 1) as i:
                for q in range(GROUPS_IN_BODY):
                    g, q1 = i * GROUPS_IN_BODY + q, (q + 1) % GROUPS_IN_BODY
                    turn_picks(g + 1, q1)
                    edge_products(i + (q1 == 0), g + 1, q1)
                    sum_messages(g, q)
            for q in range(GROUPS_IN_BODY):
                g = (ROUNDS - 1) * GROUPS_IN_BODY + q
                if q + 1 < GROUPS_IN_BODY:
                    turn_picks(g + 1, q + 1)
                    edge_products(ROUNDS - 1, g + 1, q + 1)
                sum_messages(g, q)

            with pe.Fori(0, NBATCH) as b:
                turn_batch(b + HOPS * NBATCH)
                spread_batch(b + HOPS * NBATCH)
            with pe.Fori(0, NBATCH) as b:
                n = b + (NBATCH + RBATCH)
                pe.wait_ge(p_staged, b + (NBATCH + 1))
                pe.sem_inc(pe_passed, 1)
                project(n, lambda m: stage[:, m, 0:FEAT], w_out[:, :], FEAT + 1, FEAT)

        @block.vector
        def _(dve):
            v = nc.vector
            count = [0]

            def step(ins):
                count[0] += 1
                ins.then_inc(dve_chain, 1)
                dve.wait_ge(dve_chain, count[0])

            v.memset(xs[:, NT_FULL, :], 0.0).then_inc(tail_zeroed, 1)
            dve.sem_inc(sums_added, CREDIT)
            dve.sem_inc(p_kept, CREDIT)
            dve.sem_inc(z_read, CREDIT)
            dve.sem_inc(msg_ready, CREDIT)
            dve.sem_inc(f_kept, CREDIT)
            step(v.memset(dst_before[0:1, 0:1], -1))
            step(v.memset(eps[:, :], EPS))
            dve.wait_ge(consts_made, 3)
            step(v.tensor_copy(iota[:, :], iota_i[:, :]))
            step(v.tensor_copy(part[:, 0:1], part_i[:, :]))
            step(v.tensor_copy(nbase[:, :], nbase_i[:, :]))
            step(v.tensor_scalar(part[:, 1:2], part[:, 0:1], 1.0, None, ALU.is_ge))
            step(v.tensor_scalar(part[:, 2:3], part[:, 0:1], float(P), None, ALU.mult))
            step(v.tensor_scalar(ident[:, :], iota[:, :], part[:, 0:1], None, ALU.is_equal))
            v.tensor_scalar(tri[:, :], iota[:, :], part[:, 0:1], part[:, 1:2], ALU.is_ge, ALU.mult).then_inc(tri_ready, 1)

            def layer_norm(n):
                for half, (a, z1) in enumerate(HALVES):
                    mean, hh = stats[:, 0, a:z1], h[:, a:z1, :]
                    squares = gathered[:, :, :].rearrange("p j c -> p (j c)")[:, 0:(z1 - a) * FEAT].rearrange(
                        "p (k f) -> p k f", f=FEAT)
                    step(v.tensor_reduce(mean, xs[:, a:z1, :], AX.X, ALU.add))
                    step(v.tensor_scalar(mean, mean, 1.0 / FEAT, None, ALU.mult))
                    step(v.tensor_tensor(hh, xs[:, a:z1, :], mean.unsqueeze(2).to_broadcast([P, z1 - a, FEAT]), ALU.subtract))
                    step(v.tensor_tensor(squares, hh, hh, ALU.mult))
                    v.tensor_reduce(stats[:, 1, a:z1], squares, AX.X, ALU.add).then_inc(var_ready, 1)
                    dve.wait_ge(std_ready, 2 * n + half + 1)
                    step(v.reciprocal(stats[:, 3, a:z1], stats[:, 2, a:z1]))
                    v.scalar_tensor_tensor(out=hh, in0=hh, scalar=0.0,
                                           in1=stats[:, 3, a:z1].unsqueeze(2).to_broadcast([P, z1 - a, FEAT]),
                                           op0=ALU.max, op1=ALU.mult).then_inc(h_ready, 1)

            dve.wait_ge(x_loaded, 32)
            layer_norm(0)

            dve.wait_ge(dst_loaded, 48)
            v.tensor_tensor(is_first, dst_now, dst_before, ALU.not_equal).then_inc(flags_ready, 1)
            dve.wait_ge(flags_ready, 1)
            v.tensor_tensor(first_dst[:, :], is_first, dst_now, ALU.mult).then_inc(flags_ready, 1)
            dve.wait_ge(flags_ready, 2)
            dve.wait_ge(last_loaded, 16)
            dve.wait_ge(rel_turned, 2 * len(chunks))
            step(v.tensor_scalar(is_last_below, last_dst, part[0:NT, 2:3], None, ALU.is_lt))
            step(v.tensor_reduce(small[0:NT, 1:2], is_last_below, AX.X, ALU.add))
            step(v.tensor_scalar(small[0:NT, 1:2], small[0:NT, 1:2], float(TILES - 1), None, ALU.min))
            v.tensor_copy(small_i[0:NT, 0:1], small[0:NT, 1:2]).then_inc(at_ready, 1)
            step(v.memset(ones_row, 1.0))
            dve.wait_ge(steps_ready, len(chunks))
            v.tensor_tensor_scan(base_row, ones_row, steps_row, -1.0, ALU.mult, ALU.add).then_inc(base_ready, 1)
            dve.wait_ge(base_ready, 1)
            v.tensor_copy(base_regs.rearrange("o (g e) -> o g e", e=8)[:, :, 0:GROUP],
                          base_row.rearrange("o (g e) -> o g e", e=GROUP)).then_inc(regs_ready, 1)
            dve.wait_ge(at_gathered, 32)
            step(v.tensor_scalar(below, dst_at, part[0:NT, 2:3], None, ALU.is_lt))
            step(v.tensor_tensor(differs[:, 1:P], dst_at[:, 1:P], dst_at[:, 0:P - 1], ALU.not_equal))
            step(v.memset(differs[:, 0:1], 1.0))
            step(v.tensor_tensor(below, below, differs, ALU.mult))
            step(v.tensor_reduce(small[0:NT, 2:3], below, AX.X, ALU.add))
            step(v.tensor_tensor(small[0:NT, 3:4], small[0:NT, 2:3], small[0:NT, 0:1], ALU.add))
            v.tensor_copy(small_i[0:NT, 1:2], small[0:NT, 3:4]).then_inc(first_ready, 1)
            dve.wait_ge(first_ready, 1)
            dve.wait_ge(src_loaded, 32)
            v.tensor_copy(idx[:, :], src[:, 0:BODY]).then_inc(idx_ready, GROUPS_IN_BODY)

            def next_indices(i, q):
                t = i * BODY + q * GROUP
                v.tensor_copy(idx[:, q * GROUP:(q + 1) * GROUP],
                              src[:, bass.ds(t + BODY, GROUP)]).then_inc(idx_ready, 1)

            def make_picks(i, q, s):
                t = i * BODY + q * GROUP
                for j in range(GROUP):
                    v.tensor_scalar(pick[:, s, j, :], iota[:, :], rel[:, bass.ds(t + j, 1)], None,
                                    ALU.is_equal).then_inc(pick_ready, 1)

            def load_bases(i, q):
                _, ranks = nc.values_load_multi_w_load_instructions(
                    base_regs[:, bass.ds((i * GROUPS_IN_BODY + q) * 8, GROUP)], engines=[DVE_ENGINE],
                    min_val=0, max_val=RANKS - P,
                    skip_runtime_bounds_check_because="ranks are below the number of nodes")
                return ranks

            def add_sums(phase, i, q, ranks, rows):
                n0 = ((phase * ROUNDS + i) * GROUPS_IN_BODY + q) * GROUP
                dve.wait_ge(sums_ready, n0 + (CREDIT + GROUP))
                for j in range(GROUP):
                    dve.wait_ge(sums_added, n0 + (CREDIT + j))
                    to = acc[0:rows, bass.ds(ranks[j], P)]
                    v.tensor_tensor(to, to, ps_sum[0:rows, j, :], ALU.add).then_inc(sums_added, 1)

            def stage_batch(b):
                _, ranks = nc.values_load_multi_w_load_instructions(
                    first_rank_regs[:, bass.ds(b * 8, BATCH)], engines=[DVE_ENGINE],
                    min_val=0, max_val=RANKS - P,
                    skip_runtime_bounds_check_because="ranks are at most the number of nodes")
                for m in range(BATCH):
                    ins = v.tensor_copy(stage[0:FEAT + 1, m, :], acc[0:FEAT + 1, bass.ds(ranks[m], P)])
                ins.then_inc(staged, 1)

            def make_spread(n, b):
                dve.wait_ge(turn_copied, n + 1)
                for m in range(BATCH):
                    ins = v.tensor_scalar(spread[:, m, :], iota[:, :], nbase[:, bass.ds(b * BATCH + m, 1)],
                                          turned[:, m, FEAT:FEAT + 1], ALU.add, ALU.is_equal)
                ins.then_inc(spread_ready, 1)

            dve.wait_ge(rel_copied, len(chunks))
            dve.wait_ge(first_loaded, 16)
            with dve.Fori(0, HOPS) as hop:
                v.memset(acc[0:FEAT + 1, :], 0.0).then_inc(acc_zero, 1)
                dve.wait_ge(acc_zero, hop + 1)
                dve.sem_inc(dve_passed, 1)
                with dve.Fori(0, ROUNDS) as i:
                    for q in range(GROUPS_IN_BODY):
                        make_picks(i, q, 0)
                        ranks = load_bases(i, q)
                        add_sums(hop, i, q, ranks, FEAT + 1)
                        next_indices(i, q)
                with dve.Fori(0, NBATCH) as b:
                    n = hop * NBATCH + b
                    dve.wait_ge(sums_added, (hop + 1) * TILES + CREDIT)
                    stage_batch(b)
                    make_spread(n, b)
                dve.wait_ge(staged, (hop + 1) * NBATCH)

            step(v.memset(acc[0:FEAT, :], 0.0))
            dve.wait_ge(table_ready, 16 * NBATCH * (HOPS + 1))
            step(v.tensor_tensor(xs[:, :, :], xs[:, :, :], h[:, :, :], ALU.add))
            layer_norm(1)
            dve.wait_ge(h_ready, 4)
            v.memset(turned[FEAT:FEAT + 1, :, :], 1.0).then_inc(residual_done, 1)
            dve.wait_ge(node_loaded, 16)
            step(v.tensor_copy(node_i[:, :], node_f[:, :]))

            def keep_products(n):
                dve.wait_ge(p_done, n + 1)
                dve.wait_ge(p_stored, n * 16 + 16 * CREDIT)
                v.tensor_copy(rows_out, ps_b).then_inc(p_kept, 1)

            with dve.Fori(0, NBATCH) as b:
                keep_products(b)
            with dve.Fori(0, RBATCH) as b:
                dve.wait_ge(node_used, b + CREDIT)
                v.tensor_copy(node_idx[:, :], node_i[:, bass.ds(b * BATCH, BATCH)]).then_inc(node_idx_ready, 1)
                keep_products(b + NBATCH)
            dve.wait_ge(p_stored, 16 * (CREDIT + NBATCH + RBATCH))

            def edge_sum(g, i, q):
                dve.wait_ge(z_done, g + (CREDIT + 1))
                for j in range(GROUP):
                    dve.wait_ge(gather_done[q * GROUP + j], (i + HOPS * ROUNDS) * 16 + 16)
                v.tensor_tensor(z, ps_z, gathered[:, q * GROUP:(q + 1) * GROUP, :], ALU.add).then_inc(z_ready, 1)
                dve.wait_ge(z_ready, g + 1)
                dve.sem_inc(slot_free, GROUP)
                dve.sem_inc(z_read, 1)

            def log_sums(g):
                dve.wait_ge(logs_ready, g + 1)
                v.scalar_tensor_tensor(out=lg[:, :, 0:FEAT], in0=z[:, :, 0:FEAT], scalar=0.0, in1=lg[:, :, 0:FEAT],
                                       op0=ALU.min, op1=ALU.subtract).then_inc(gate_arg, 1)
                v.scalar_tensor_tensor(out=lg[:, :, FEAT:F2], in0=z[:, :, FEAT:F2], scalar=0.0, in1=lg[:, :, FEAT:F2],
                                       op0=ALU.max, op1=ALU.add).then_inc(soft_ready, 1)
                dve.wait_ge(gate_arg, g + 1)
                dve.wait_ge(soft_ready, g + 1)

            def messages(g):
                dve.wait_ge(gate_ready, g + 1)
                v.tensor_tensor(msg[:, :, 0:FEAT], lg[:, :, 0:FEAT], lg[:, :, FEAT:F2], ALU.mult).then_inc(msg_ready, 1)

            make_picks(0, 0, SLOT3[0])
            edge_sum(0, 0, 0)
            with dve.Fori(0, ROUNDS - 1) as i:
                for q in range(GROUPS_IN_BODY):
                    g, q1 = i * GROUPS_IN_BODY + q, (q + 1) % GROUPS_IN_BODY
                    i1 = i + (q1 == 0)
                    make_picks(i1, q1, SLOT3[q1])
                    log_sums(g)
                    edge_sum(g + 1, i1, q1)
                    messages(g)
                    next_indices(i, q)
                    add_sums(HOPS, i, q, load_bases(i, q), FEAT)
            for q in range(GROUPS_IN_BODY):
                i = ROUNDS - 1
                g = i * GROUPS_IN_BODY + q
                if q + 1 < GROUPS_IN_BODY:
                    make_picks(i, q + 1, SLOT3[q + 1])
                log_sums(g)
                if q + 1 < GROUPS_IN_BODY:
                    edge_sum(g + 1, i, q + 1)
                messages(g)
                add_sums(HOPS, i, q, load_bases(i, q), FEAT)

            dve.wait_ge(sums_added, (HOPS + 1) * TILES + CREDIT)
            with dve.Fori(0, NBATCH) as b:
                n = b + HOPS * NBATCH
                stage_batch(b)
                make_spread(n, b)
                dve.wait_ge(batch_done, n + 1)
                to = h[:, bass.ds(b * BATCH, BATCH), :]
                v.tensor_tensor(to, to, ps_b[:, :, 0:FEAT], ALU.add).then_inc(batch_kept, 1)
            dve.wait_ge(batch_kept, (HOPS + 1) * NBATCH)
            v.memset(turned[FEAT:FEAT + 1, :, :], 1.0).then_inc(residual_done, 1)
            with dve.Fori(0, NBATCH) as b:
                n = b + (NBATCH + RBATCH)
                dve.wait_ge(p_done, n + 1)
                dve.wait_ge(out_stored, b * 16 + 16 * CREDIT)
                v.scalar_tensor_tensor(out=rows_out[:, :, 0:FEAT], in0=ps_b[:, :, 0:FEAT], scalar=0.0,
                                       in1=xs[:, bass.ds(b * BATCH, BATCH), :],
                                       op0=ALU.max, op1=ALU.add).then_inc(f_kept, 1)
                dve.wait_ge(f_kept, b + (CREDIT + 1))
                dve.sem_inc(p_kept, 1)


def kernel(x, src, dst, edge_attr_32, edge_weight, L1_gnn_Wf, L1_gnn_bf, L1_gnn_Ws, L1_gnn_bs, L1_gnn_Wm, L1_gnn_bm):
    import numpy as np
    import concourse.bacc as bacc
    from concourse.bass_utils import run_bass_kernel_spmd

    def cols(a):
        return np.ascontiguousarray(np.asarray(a).reshape(-1, P).T)

    arrays = {
        "x": np.ascontiguousarray(x),
        "src_t": cols(src),
        "dst_t": cols(dst),
        "dst_rows": np.ascontiguousarray(np.asarray(dst).reshape(-1, P)),
        "w_t": cols(edge_weight),
        "attr_t": np.ascontiguousarray(np.asarray(edge_attr_32).T),
        "w_f": np.ascontiguousarray(L1_gnn_Wf),
        "w_s": np.ascontiguousarray(L1_gnn_Ws),
        "b_f": np.ascontiguousarray(L1_gnn_bf).reshape(1, -1),
        "b_s": np.ascontiguousarray(L1_gnn_bs).reshape(1, -1),
        "w_m": np.ascontiguousarray(L1_gnn_Wm),
        "b_m": np.ascontiguousarray(L1_gnn_bm).reshape(1, -1),
    }
    nc = bacc.Bacc("TRN2", target_bir_lowering=False, num_devices=1)
    args = [nc.dram_tensor(name, a.shape, mybir.dt.from_np(a.dtype), kind="ExternalInput").ap()
            for name, a in arrays.items()]
    out = nc.dram_tensor("out", arrays["x"].shape, F32, kind="ExternalOutput").ap()
    build(nc, *args, out)
    r = run_bass_kernel_spmd(nc, [arrays], core_ids=[0])
    return r.results[0]["out"]
```

```python
from contextlib import ExitStack

import concourse.bass as bass
from concourse import mybir

P = 128
F32 = mybir.dt.float32
BF16 = mybir.dt.bfloat16
I32 = mybir.dt.int32
ALU = mybir.AluOpType
ACT = mybir.ActivationFunctionType
AX = mybir.AxisListType
DVE_ENGINE = mybir.EngineType.DVE
SP_ENGINE = mybir.EngineType.SP

HOPS = 3
GROUP = 5
GROUPS_IN_BODY = 5
CONV_BODY = 10
BATCH = 7
EPS = 1e-5


def build(nc, x, src_t, dst_t, dst_rows, w_t, attr_t, w_f, w_s, b_f, b_s, w_m, b_m, out):
    NODES, FEAT = x.shape
    TILES = src_t.shape[1]
    EDIM = attr_t.shape[0]
    BODY = GROUP * GROUPS_IN_BODY
    ROUNDS = TILES // BODY
    GROUPS = TILES // GROUP
    NT = -(-NODES // P)
    NT_FULL = NODES // P
    NREST = NODES - NT_FULL * P
    NBATCH = NT // BATCH
    RT = -(-(NODES + P) // (P * BATCH)) * BATCH
    RBATCH = RT // BATCH
    RANKS = RT * P
    F2 = 2 * FEAT
    HALVES = [(0, NT // 2), (NT // 2, NT)]
    chunks = [(a, min(a + 512, TILES)) for a in range(0, TILES, 512)]
    assert dst_t.shape[0] == P and TILES % BODY == 0 and NT % BATCH == 0 and FEAT == 64

    CREDIT = BODY

    CONV_ROUNDS = (GROUPS - 1) // CONV_BODY
    TAIL = range(1, GROUPS - CONV_ROUNDS * CONV_BODY)
    assert CONV_BODY % GROUPS_IN_BODY == 0 and CONV_BODY % 2 == 0

    ctx = ExitStack()
    with ctx:
        def sb(name, shape, dt=F32):
            return ctx.enter_context(nc.sbuf_tensor(name, shape, dt))

        def sem(name):
            return ctx.enter_context(nc.semaphore(name))

        def dram(name, shape, dt=F32):
            return nc.dram_tensor(name, shape, dt, kind="Internal").ap()

        h_table = dram("h_table", (NT * P, FEAT))
        src_table = dram("src_table", (NT * P, F2))
        dst_by_rank = dram("dst_by_rank", (RANKS, 3 * F2), BF16)
        base_dram = dram("base_dram", (TILES, 1))
        first_rank_dram = dram("first_rank_dram", (NT, 1), I32)
        node_dram = dram("node_dram", (RANKS, 1))

        acc = sb("acc", [P, RANKS])
        xs = sb("xs", [P, NT, FEAT])
        h = sb("h", [P, NT, FEAT])
        src = sb("src", [P, TILES + BODY], I32)
        w = sb("w", [P, TILES])
        rel = sb("rel", [P, TILES])
        first_dst = sb("first_dst", [P, TILES])
        gathered = sb("gathered", [P, BODY, F2])
        idx = sb("idx", [P, BODY], I32)
        msg = sb("msg", [P, 2, GROUP, FEAT + 1])
        pick = sb("pick", [P, GROUPS_IN_BODY, GROUP, P])
        iota = sb("iota", [P, P])
        part = sb("part", [P, 4])
        nbase = sb("nbase", [P, NT])
        ident = sb("ident", [P, P])
        tri = sb("tri", [P, P])
        stats = sb("stats", [P, 4, NT])
        eps = sb("eps", [P, 1])
        small = sb("small", [P, 8])
        small_i = sb("small_i", [P, 2], I32)
        node_f = sb("node_f", [P, RT])
        node_i = sb("node_i", [P, RT], I32)
        node_idx = sb("node_idx", [P, BATCH], I32)
        w_src = sb("w_src", [FEAT, F2])
        w_dst = sb("w_dst", [FEAT + 1, F2])
        w_edge = sb("w_edge", [EDIM, F2])
        w_out = sb("w_out", [FEAT + 1, FEAT])

        scratch = sb("scratch", [P, 4 * BATCH * P])
        in_batch = scratch[:, :].rearrange("p (n m c) -> p n m c", n=4, m=BATCH)
        stage, turned, spread, rows_out = (in_batch[:, n] for n in range(4))
        G1 = GROUP * P
        in_group = scratch[:, 0:4 * G1].rearrange("p (n j c) -> p n j c", n=4, j=GROUP)
        z, e, lg = (in_group[:, n] for n in range(3))
        pick_t = scratch[:, 3 * G1:3 * G1 + G1 // 2].bitcast(BF16).rearrange("p (j c) -> p j c", j=GROUP)
        rest = stage
        parts_out = scratch[:, 2 * BATCH * P:2 * BATCH * P + 3 * BATCH * P // 2].bitcast(BF16).rearrange(
            "p (m n c) -> p m n c", m=BATCH, n=3)
        iota_i = scratch[:, 0:P].bitcast(I32)
        nbase_i = scratch[:, P:P + NT].bitcast(I32)
        part_i = scratch[:, 2 * P:2 * P + 1].bitcast(I32)
        q_win = w[:, 0:2 * GROUP * 3 * F2 // 2].bitcast(BF16).rearrange("p (s j c) -> p s j c", s=2, j=GROUP)
        attr = sb("attr", [EDIM, 2, GROUP * P])

        psum = ctx.enter_context(nc.psum_tensor("psum", [P, 8 * 512], F32))
        ps_sums = [psum[:, a:a + G1].rearrange("p (j c) -> p j c", j=GROUP) for a in (0, 1024)]
        ps_turn = psum[:, 2048:2048 + G1].rearrange("p (j c) -> p j c", j=GROUP)
        ps_z = psum[:, 3072:3072 + G1].rearrange("p (j c) -> p j c", j=GROUP)
        ps_a = psum[:, 0:BATCH * P].rearrange("p (m c) -> p m c", m=BATCH)
        ps_b = psum[:, 1024:1024 + BATCH * P].rearrange("p (m c) -> p m c", m=BATCH)

        dst_now = acc[:, 0:TILES].bitcast(I32)
        dst_before = acc[:, TILES:2 * TILES].bitcast(I32)
        is_first = acc[:, 2 * TILES:3 * TILES]
        last_dst = acc[0:NT, 3 * TILES:4 * TILES].bitcast(I32)
        ROW = 96
        steps_row = acc[ROW:ROW + 1, 0:TILES]
        ones_row = acc[ROW:ROW + 1, TILES:2 * TILES]
        base_row = acc[ROW:ROW + 1, 2 * TILES:3 * TILES]
        base_regs = acc[ROW:ROW + 1, 0:8 * GROUPS].bitcast(I32)
        first_rank_regs = acc[ROW:ROW + 1, 8 * GROUPS:8 * GROUPS + 8 * NBATCH].bitcast(I32)
        dst_at = scratch[0:NT, 0:P].bitcast(I32)
        below = scratch[0:NT, P:2 * P]
        differs = scratch[0:NT, 2 * P:3 * P]
        is_last_below = acc[0:NT, 2 * TILES:3 * TILES]

        pool_passed = sem("pool_passed")
        pe_passed = sem("pe_passed")
        dve_passed = sem("dve_passed")
        consts_made = sem("consts_made")
        x_loaded = sem("x_loaded")
        dst_loaded = sem("dst_loaded")
        dst_shifted = sem("dst_shifted")
        before_set = sem("before_set")
        last_loaded = sem("last_loaded")
        src_loaded = sem("src_loaded")
        w_loaded = sem("w_loaded")
        weights_loaded = sem("weights_loaded")
        dve_chain = sem("dve_chain")
        tail_zeroed = sem("tail_zeroed")
        var_ready = sem("var_ready")
        std_ready = sem("std_ready")
        h_ready = sem("h_ready")
        table_ready = sem("table_ready")
        tri_ready = sem("tri_ready")
        flags_ready = sem("flags_ready")
        rel_turned = sem("rel_turned")
        rel_copied = sem("rel_copied")
        steps_ready = sem("steps_ready")
        base_ready = sem("base_ready")
        base_stored = sem("base_stored")
        at_ready = sem("at_ready")
        at_gathered = sem("at_gathered")
        first_ready = sem("first_ready")
        first_stored = sem("first_stored")
        first_loaded = sem("first_loaded")
        regs_ready = sem("regs_ready")
        idx_ready = sem("idx_ready")
        gather_done = [sem(f"gather_done_{j}") for j in range(BODY)]
        slot_free = sem("slot_free")
        pick_ready = sem("pick_ready")
        sums_ready = sem("sums_ready")
        sums_added = sem("sums_added")
        staged = sem("staged")
        acc_zero = sem("acc_zero")
        turn_done = sem("turn_done")
        turn_copied = sem("turn_copied")
        spread_ready = sem("spread_ready")
        batch_done = sem("batch_done")
        batch_kept = sem("batch_kept")
        residual_done = sem("residual_done")
        node_stored = sem("node_stored")
        node_loaded = sem("node_loaded")
        node_idx_ready = sem("node_idx_ready")
        node_rows = [sem(f"node_rows_{m}") for m in range(BATCH)]
        node_used = sem("node_used")
        p_staged = sem("p_staged")
        p_turned = sem("p_turned")
        p_copied = sem("p_copied")
        p_done = sem("p_done")
        p_kept = sem("p_kept")
        p_stored = sem("p_stored")
        split_steps = sem("split_steps")
        group_loaded = [sem(f"group_loaded_{s}") for s in range(2)]
        pick_turned = sem("pick_turned")
        pick_t_ready = sem("pick_t_ready")
        z_done = sem("z_done")
        z_ready = sem("z_ready")
        z_read = sem("z_read")
        gate_arg = sem("gate_arg")
        soft_ready = sem("soft_ready")
        logs_ready = sem("logs_ready")
        act_steps = sem("act_steps")
        gate_ready = sem("gate_ready")
        msg_ready = sem("msg_ready")
        conv_sums = sem("conv_sums")
        conv_added = sem("conv_added")
        f_kept = sem("f_kept")
        out_stored = sem("out_stored")

        h_table_v = h_table.rearrange("(k p) f -> p k f", p=P)
        src_table_v = src_table.rearrange("(k p) f -> p k f", p=P)
        rank_v = dst_by_rank.rearrange("(p j) (n f) -> p j n f", p=P, n=3)

        block = ctx.enter_context(nc.Block())

        @block.sync
        def _(sp):
            sp.wait_ge(tail_zeroed, 1)
            sp.dma_start(xs[:, 0:NT_FULL, :], x[0:NT_FULL * P].rearrange("(k p) f -> p k f", p=P)).then_inc(x_loaded, 16)
            sp.dma_start(xs[0:NREST, NT_FULL, :], x[NT_FULL * P:NODES]).then_inc(x_loaded, 16)
            sp.dma_start(src[:, 0:TILES], src_t).then_inc(src_loaded, 16)
            sp.dma_start(src[:, TILES:TILES + BODY], src_t[:, 0:BODY]).then_inc(src_loaded, 16)
            sp.dma_start(w[:, :], w_t).then_inc(w_loaded, 16)
            for dst_ap, a in ((w_dst[0:FEAT], (0, FEAT)), (w_src[:], (FEAT, F2)), (w_edge[:], (F2, F2 + EDIM))):
                sp.dma_start(dst_ap[:, 0:FEAT], w_f[a[0]:a[1]]).then_inc(weights_loaded, 16)
                sp.dma_start(dst_ap[:, FEAT:F2], w_s[a[0]:a[1]]).then_inc(weights_loaded, 16)
            sp.dma_start(w_dst[FEAT:FEAT + 1, 0:FEAT], b_f).then_inc(weights_loaded, 16)
            sp.dma_start(w_dst[FEAT:FEAT + 1, FEAT:F2], b_s).then_inc(weights_loaded, 16)
            sp.dma_start(w_out[0:FEAT, :], w_m).then_inc(weights_loaded, 16)
            sp.dma_start(w_out[FEAT:FEAT + 1, :], b_m).then_inc(weights_loaded, 16)

            for n, (a, z1) in enumerate(HALVES):
                sp.wait_ge(h_ready, n + 1)
                sp.dma_start(h_table_v[:, a:z1, :], h[:, a:z1, :]).then_inc(table_ready, 8 * NBATCH)

            sp.wait_ge(base_ready, 1)
            sp.dma_start(base_dram.rearrange("t o -> o t"), base_row).then_inc(base_stored, 16)
            sp.wait_ge(first_ready, 1)
            sp.dma_start(first_rank_dram, small_i[0:NT, 1:2]).then_inc(first_stored, 16)
            sp.wait_ge(first_stored, 16)
            sp.wait_ge(regs_ready, 1)
            sp.dma_start(first_rank_regs.rearrange("o (b e) -> o b e", e=8)[:, :, 0:BATCH],
                         first_rank_dram.rearrange("(b e) o -> o b e", e=BATCH)).then_inc(first_loaded, 16)

            with sp.Fori(0, HOPS) as hop:
                with sp.Fori(0, NBATCH) as b:
                    sp.wait_ge(batch_kept, hop * NBATCH + b + 1)
                    sp.dma_start(h_table_v[:, bass.ds(b * BATCH, BATCH), :],
                                 h[:, bass.ds(b * BATCH, BATCH), :]).then_inc(table_ready, 16)

            sp.wait_ge(batch_kept, HOPS * NBATCH)
            sp.dma_start(node_dram.rearrange("r o -> o r"), acc[FEAT:FEAT + 1, :]).then_inc(node_stored, 16)
            sp.wait_ge(node_stored, 16)
            sp.dma_start(node_f[:, :], node_dram.rearrange("(p j) o -> p (j o)", p=P)).then_inc(node_loaded, 16)
            sp.wait_ge(table_ready, 16 * NBATCH * (HOPS + 1))
            for n, (a, z1) in enumerate(HALVES):
                sp.wait_ge(h_ready, n + 3)
                sp.dma_start(h_table_v[:, a:z1, :], h[:, a:z1, :]).then_inc(table_ready, 8 * NBATCH)
            with sp.Fori(0, NBATCH) as b:
                sp.wait_ge(p_kept, CREDIT + b + 1)
                sp.dma_start(src_table_v[:, bass.ds(b * BATCH, BATCH), :], rows_out).then_inc(p_stored, 16)
            with sp.Fori(0, RBATCH) as b:
                sp.wait_ge(p_kept, b + (CREDIT + NBATCH + 1))
                sp.dma_start(rank_v[:, bass.ds(b * BATCH, BATCH), :, :], parts_out).then_inc(p_stored, 16)
            sp.wait_ge(p_stored, CREDIT * 16 + 16 * (NBATCH + RBATCH))

            def load_group(g, s):
                _, ranks = nc.values_load_multi_w_load_instructions(
                    base_regs[:, bass.ds(g * 8, GROUP)], engines=[SP_ENGINE], min_val=0, max_val=RANKS - P,
                    skip_runtime_bounds_check_because="ranks are below the number of nodes")
                sp.wait_ge(z_done, g + (CREDIT - 1))
                sp.dma_start(attr[:, s, :], attr_t[:, bass.ds(g * (GROUP * P), GROUP * P)]).then_inc(group_loaded[s], 16)
                for j in range(GROUP):
                    sp.dma_start(q_win[:, s, j, :], dst_by_rank[bass.ds(ranks[j], P), :]).then_inc(group_loaded[s], 16)

            with sp.Fori(0, GROUPS // 2) as i:
                for s in range(2):
                    load_group(i * 2 + s, s)
            if GROUPS % 2:
                load_group(GROUPS - 1, 0)

            with sp.Fori(0, NBATCH - 1) as b:
                sp.wait_ge(f_kept, b + (CREDIT + 1))
                sp.dma_start(out[bass.ds(b * (BATCH * P), BATCH * P), :].rearrange("(k p) f -> p k f", p=P),
                             rows_out[:, :, 0:FEAT]).then_inc(out_stored, 16)
            sp.wait_ge(f_kept, CREDIT + NBATCH)
            last = (NBATCH - 1) * BATCH * P
            sp.dma_start(out[last:NT_FULL * P, :].rearrange("(k p) f -> p k f", p=P),
                         rows_out[:, 0:BATCH - 1, 0:FEAT]).then_inc(out_stored, 16)
            sp.dma_start(out[NT_FULL * P:NODES, :], rows_out[0:NREST, BATCH - 1, 0:FEAT]).then_inc(out_stored, 16)
            sp.wait_ge(out_stored, 16 * (CREDIT + NBATCH + 1))

        @block.gpsimd
        def _(pool):
            nc.gpsimd.iota(iota_i[:, :], pattern=[[1, P]], base=0, channel_multiplier=0).then_inc(consts_made, 1)
            nc.gpsimd.iota(part_i[:, :], pattern=[[0, 1]], base=0, channel_multiplier=1).then_inc(consts_made, 1)
            nc.gpsimd.iota(nbase_i[:, :], pattern=[[P, NT]], base=0, channel_multiplier=0).then_inc(consts_made, 1)

            def gather(out_ap, table, index, done):
                pool.indirect_dma_start(out=out_ap, out_offset=None, in_=table,
                                        in_offset=bass.IndirectOffsetOnAxis(ap=index, axis=0)).then_inc(done, 16)

            pool.wait_ge(at_ready, 1)
            pool.wait_ge(base_stored, 16)
            gather(dst_at, dst_rows, small_i[0:NT, 0:1], at_gathered)
            gather(small[0:NT, 0:1], base_dram, small_i[0:NT, 0:1], at_gathered)

            def gather_group(phase, i, q, table, width):
                g = (phase * ROUNDS + i) * GROUPS_IN_BODY + q
                pool.wait_ge(idx_ready, g + 1)
                pool.wait_ge(slot_free, g * GROUP + GROUP)
                pool.sem_inc(pool_passed, 1)
                for j in range(GROUP):
                    k = q * GROUP + j
                    gather(gathered[:, k, 0:width], table, idx[:, k:k + 1], gather_done[k])

            with pool.Fori(0, HOPS) as hop:
                pool.wait_ge(table_ready, (hop + 1) * (16 * NBATCH))
                pool.sem_inc(pool_passed, 1)
                with pool.Fori(0, ROUNDS) as i:
                    for q in range(GROUPS_IN_BODY):
                        gather_group(hop, i, q, h_table, FEAT)

            pool.wait_ge(table_ready, 16 * NBATCH * (HOPS + 2))
            with pool.Fori(0, RBATCH) as b:
                pool.wait_ge(node_idx_ready, b + 1)
                pool.wait_ge(node_used, b + CREDIT)
                pool.sem_inc(pool_passed, 1)
                for m in range(BATCH):
                    gather(gathered[:, m, 0:FEAT], h_table, node_idx[:, m:m + 1], node_rows[m])

            pool.wait_ge(p_stored, 16 * (CREDIT + NBATCH))
            pool.wait_ge(node_used, RBATCH + CREDIT)
            with pool.Fori(0, ROUNDS) as i:
                for q in range(GROUPS_IN_BODY):
                    gather_group(HOPS, i, q, src_table, F2)

        @block.scalar
        def _(act):
            act.sem_inc(slot_free, CREDIT)
            act.sem_inc(p_stored, 16 * CREDIT)
            act.sem_inc(out_stored, 16 * CREDIT)
            act.dma_start(dst_now, dst_t).then_inc(dst_loaded, 16)
            act.dma_start(dst_before[1:P, :], dst_t[0:P - 1, :]).then_inc(dst_loaded, 16)
            act.dma_start(dst_before[0:1, 1:TILES], dst_t[P - 1:P, 0:TILES - 1]).then_inc(dst_loaded, 16)
            act.dma_start(last_dst, dst_t[P - 1:P, :].to_broadcast([NT, TILES])).then_inc(last_loaded, 16)

            def std(n):
                a, z1 = HALVES[(n - 1) % 2]
                act.wait_ge(var_ready, n)
                nc.scalar.activation(stats[:, 2, a:z1], stats[:, 1, a:z1], ACT.Sqrt, bias=eps[:, :],
                                     scale=1.0 / FEAT).then_inc(std_ready, 1)

            std(1)
            std(2)
            for n, (a, z1) in enumerate(chunks):
                act.wait_ge(rel_turned, n + 1)
                nc.scalar.copy(rel[:, a:z1], psum[:, n * 512:n * 512 + z1 - a]).then_inc(rel_copied, 1)
            act.wait_ge(flags_ready, 2)
            for n, (a, z1) in enumerate(chunks):
                act.wait_ge(rel_turned, len(chunks) + n + 1)
                nc.scalar.copy(steps_row[:, a:z1], psum[0:1, n * 512:n * 512 + z1 - a]).then_inc(steps_ready, 1)

            def scale_group(phase, i, q):
                r = phase * ROUNDS + i
                g = r * GROUPS_IN_BODY + q
                t = i * BODY + q * GROUP
                act.wait_ge(sums_ready, g * GROUP + CREDIT)
                nc.scalar.copy(msg[:, 0, :, FEAT], first_dst[:, bass.ds(t, GROUP)])
                for j in range(GROUP):
                    k = q * GROUP + j
                    act.wait_ge(gather_done[k], r * 16 + 16)
                    nc.scalar.activation(msg[:, 0, j, 0:FEAT], gathered[:, k, 0:FEAT], ACT.Copy,
                                         scale=w[:, bass.ds(t + j, 1)]).then_inc(slot_free, 1)

            def copy_turned(n):
                act.wait_ge(turn_done, n + 1)
                nc.scalar.copy(turned[:, :, 0:FEAT + 1], ps_a[:, :, 0:FEAT + 1]).then_inc(turn_copied, 1)

            act.wait_ge(w_loaded, 16)
            act.wait_ge(flags_ready, 2)
            with act.Fori(0, HOPS) as hop:
                with act.Fori(0, ROUNDS) as i:
                    for q in range(GROUPS_IN_BODY):
                        scale_group(hop, i, q)
                with act.Fori(0, NBATCH) as b:
                    n = hop * NBATCH + b
                    copy_turned(n)
                    act.wait_ge(batch_done, n + 1)
                    nc.scalar.copy(h[:, bass.ds(b * BATCH, BATCH), :], ps_b[:, :, 0:FEAT]).then_inc(batch_kept, 1)

            std(3)
            std(4)

            def copy_project(n, width):
                act.wait_ge(p_turned, n + (CREDIT + 1))
                nc.scalar.copy(turned[0:FEAT, :, :], ps_a[0:FEAT, :, :]).then_inc(p_copied, 1)

            act.wait_ge(h_ready, 4)
            with act.Fori(0, NBATCH) as b:
                act.wait_ge(p_turned, b + CREDIT)
                nc.scalar.copy(stage[:, :, 0:FEAT], h[:, bass.ds(b * BATCH, BATCH), :]).then_inc(p_staged, 1)
                copy_project(b, F2)
            with act.Fori(0, RBATCH) as b:
                copy_project(b + NBATCH, F2)

            def turn_pick(g):
                act.wait_ge(pick_turned, g + 1)
                nc.scalar.copy(pick_t, ps_turn).then_inc(pick_t_ready, 1)

            def gate_of(g):
                act.wait_ge(gate_arg, g + 1)
                nc.scalar.activation(lg[:, :, 0:FEAT], lg[:, :, 0:FEAT], ACT.Exp).then_inc(gate_ready, 1)

            def log_terms(g):
                act.wait_ge(z_ready, g + 1)
                nc.scalar.activation(e, z, ACT.Abs).then_inc(act_steps, 1)
                act.wait_ge(act_steps, g * 2 + 1)
                nc.scalar.activation(e, e, ACT.Exp, scale=-1.0).then_inc(act_steps, 1)
                act.wait_ge(act_steps, g * 2 + 2)
                act.wait_ge(msg_ready, g + CREDIT)
                nc.scalar.activation(lg, e, ACT.Ln, bias=1.0).then_inc(logs_ready, 1)

            def conv_step(i, o):
                g = i * CONV_BODY + o
                if not isinstance(i, int) or g + 2 < GROUPS:
                    turn_pick(g + 2)
                gate_of(g)
                if not isinstance(i, int) or g + 1 < GROUPS:
                    log_terms(g + 1)

            nc.scalar.preload_act_table_set("natural_log_exp_and_others")
            turn_pick(0)
            turn_pick(1)
            log_terms(0)
            conv_step(0, 0)
            with act.Fori(0, CONV_ROUNDS) as i:
                for o in range(1, CONV_BODY + 1):
                    conv_step(i, o)
            for o in TAIL:
                conv_step(CONV_ROUNDS, o)

            with act.Fori(0, NBATCH) as b:
                copy_turned(b + HOPS * NBATCH)
            act.wait_ge(residual_done, 2)
            with act.Fori(0, NBATCH) as b:
                n = b + (NBATCH + RBATCH)
                act.wait_ge(p_turned, n + CREDIT)
                nc.scalar.copy(stage[:, :, 0:FEAT], h[:, bass.ds(b * BATCH, BATCH), :]).then_inc(p_staged, 1)
                copy_project(n, FEAT)

        @block.tensor
        def _(pe):
            pe.sem_inc(sums_ready, CREDIT)
            pe.sem_inc(p_turned, CREDIT)
            pe.sem_inc(z_done, CREDIT)
            pe.sem_inc(node_used, CREDIT)
            pe.wait_ge(tri_ready, 1)
            pe.wait_ge(flags_ready, 1)
            for n, (a, z1) in enumerate(chunks):
                pe.matmul(psum[:, n * 512:n * 512 + z1 - a], tri[:, :], is_first[:, a:z1],
                          start=True, stop=True).then_inc(rel_turned, 1)
            for n, (a, z1) in enumerate(chunks):
                pe.wait_ge(rel_copied, n + 1)
                if a == 0:
                    pe.matmul(psum[0:1, 0:1], ident[:, 0:1], is_first[:, 0:1], start=True, stop=True)
                    pe.matmul(psum[0:1, 1:z1], ident[:, 0:1], is_first[:, 1:z1], start=True, stop=False)
                    pe.matmul(psum[0:1, 1:z1], tri[:, P - 1:P], is_first[:, 0:z1 - 1],
                              start=False, stop=True).then_inc(rel_turned, 1)
                else:
                    to = psum[0:1, n * 512:n * 512 + z1 - a]
                    pe.matmul(to, ident[:, 0:1], is_first[:, a:z1], start=True, stop=False)
                    pe.matmul(to, tri[:, P - 1:P], is_first[:, a - 1:z1 - 1],
                              start=False, stop=True).then_inc(rel_turned, 1)

            pe.wait_ge(steps_ready, len(chunks))

            def sum_group(phase, i, q):
                n0 = ((phase * ROUNDS + i) * GROUPS_IN_BODY + q) * GROUP
                pe.wait_ge(sums_added, n0 + CREDIT)
                for j in range(GROUP):
                    pe.wait_ge(slot_free, n0 + (CREDIT + j + 1))
                    pe.wait_ge(pick_ready, n0 + (j + 1))
                    pe.matmul(ps_sums[0][0:FEAT + 1, j, :], msg[:, 0, j, :], pick[:, 0, j, :],
                              start=True, stop=True).then_inc(sums_ready, 1)

            def turn_batch(n):
                pe.wait_ge(staged, n + 1)
                for m in range(BATCH):
                    mm = pe.transpose(ps_a[:, m, 0:FEAT + 1], stage[0:FEAT + 1, m, :], ident[0:FEAT + 1, 0:FEAT + 1])
                mm.then_inc(turn_done, 1)

            def spread_batch(n):
                pe.wait_ge(spread_ready, n + 1)
                for m in range(BATCH):
                    mm = pe.matmul(ps_b[:, m, 0:FEAT], spread[:, m, :], turned[:, m, 0:FEAT], start=True, stop=True)
                mm.then_inc(batch_done, 1)

            with pe.Fori(0, HOPS) as hop:
                with pe.Fori(0, ROUNDS) as i:
                    for q in range(GROUPS_IN_BODY):
                        sum_group(hop, i, q)
                with pe.Fori(0, NBATCH) as b:
                    n = hop * NBATCH + b
                    turn_batch(n)
                    spread_batch(n)

            def project(n, rows, weights, k, width):
                for m in range(BATCH):
                    mm = pe.transpose(ps_a[0:FEAT, m, :], rows(m), ident[:, :])
                mm.then_inc(p_turned, 1)
                pe.wait_ge(p_copied, n + 1)
                pe.wait_ge(p_kept, n + CREDIT)
                for m in range(BATCH):
                    mm = pe.matmul(ps_b[:, m, 0:width], turned[0:k, m, :], weights, start=True, stop=True)
                mm.then_inc(p_done, 1)

            pe.wait_ge(weights_loaded, 16 * 10)
            pe.wait_ge(residual_done, 1)
            with pe.Fori(0, NBATCH) as b:
                pe.wait_ge(p_staged, b + 1)
                pe.sem_inc(pe_passed, 1)
                project(b, lambda m: stage[:, m, 0:FEAT], w_src[:, :], FEAT, F2)
            with pe.Fori(0, RBATCH) as b:
                for m in range(BATCH):
                    pe.wait_ge(node_rows[m], b * 16 + 16)
                pe.sem_inc(pe_passed, 1)
                n = b + NBATCH
                for m in range(BATCH):
                    mm = pe.transpose(ps_a[0:FEAT, m, :], gathered[:, m, 0:FEAT], ident[:, :])
                mm.then_inc(p_turned, 1)
                pe.wait_ge(p_copied, n + 1)
                pe.sem_inc(node_used, 1)
                pe.wait_ge(p_kept, n + CREDIT)
                for m in range(BATCH):
                    mm = pe.matmul(ps_b[:, m, :], turned[0:FEAT + 1, m, :], w_dst[:, :], start=True, stop=True)
                mm.then_inc(p_done, 1)
            pe.wait_ge(p_kept, CREDIT + NBATCH + RBATCH)

            PHASE0 = HOPS * TILES

            def turn_picks(i, o):
                g = i * CONV_BODY + o
                pe.wait_ge(pick_ready, g * GROUP + (PHASE0 + GROUP))
                for j in range(GROUP):
                    mm = pe.transpose(ps_turn[:, j, :], pick[:, o % GROUPS_IN_BODY, j, :], ident[:, :])
                mm.then_inc(pick_turned, 1)

            def edge_products(i, o):
                g, s = i * CONV_BODY + o, o % 2
                pe.wait_ge(pick_t_ready, g + 1)
                pe.wait_ge(group_loaded[s], (i * (CONV_BODY // 2) + (o // 2 + 1)) * (16 * (GROUP + 1)))
                pe.wait_ge(z_read, g + CREDIT)
                for j in range(GROUP):
                    for n in range(3):
                        pe.matmul(ps_z[:, j, :], pick_t[:, j, :], q_win[:, s, j, n * F2:(n + 1) * F2],
                                  start=(n == 0), stop=False)
                    mm = pe.matmul(ps_z[:, j, :], attr[:, s, j * P:(j + 1) * P], w_edge[:, :], start=False, stop=True)
                mm.then_inc(z_done, 1)

            def sum_messages(i, o):
                g, s = i * CONV_BODY + o, o % 2
                pe.wait_ge(msg_ready, g + (CREDIT + 1))
                pe.wait_ge(sums_added, g * GROUP + (PHASE0 + CREDIT - GROUP))
                for j in range(GROUP):
                    pe.matmul(ps_sums[s][0:FEAT, j, :], msg[:, s, j, 0:FEAT], pick[:, o % GROUPS_IN_BODY, j, :],
                              start=True, stop=True).then_inc(sums_ready, 1)

            def conv_step(i, o):
                if not isinstance(i, int) or i * CONV_BODY + o + 2 < GROUPS:
                    turn_picks(i, o + 2)
                    edge_products(i, o + 2)
                sum_messages(i, o)

            for g in range(2):
                turn_picks(0, g)
                edge_products(0, g)
            conv_step(0, 0)
            with pe.Fori(0, CONV_ROUNDS) as i:
                for o in range(1, CONV_BODY + 1):
                    conv_step(i, o)
            for o in TAIL:
                conv_step(CONV_ROUNDS, o)

            with pe.Fori(0, NBATCH) as b:
                turn_batch(b + HOPS * NBATCH)
                spread_batch(b + HOPS * NBATCH)
            with pe.Fori(0, NBATCH) as b:
                n = b + (NBATCH + RBATCH)
                pe.wait_ge(p_staged, b + (NBATCH + 1))
                pe.sem_inc(pe_passed, 1)
                project(n, lambda m: stage[:, m, 0:FEAT], w_out[:, :], FEAT + 1, FEAT)

        @block.vector
        def _(dve):
            v = nc.vector
            count = [0]

            def step(ins):
                count[0] += 1
                ins.then_inc(dve_chain, 1)
                dve.wait_ge(dve_chain, count[0])

            v.memset(xs[:, NT_FULL, :], 0.0).then_inc(tail_zeroed, 1)
            dve.sem_inc(sums_added, CREDIT)
            dve.sem_inc(p_kept, CREDIT)
            dve.sem_inc(z_read, CREDIT)
            dve.sem_inc(msg_ready, CREDIT)
            dve.sem_inc(f_kept, CREDIT)
            step(v.memset(dst_before[0:1, 0:1], -1))
            step(v.memset(eps[:, :], EPS))
            dve.wait_ge(consts_made, 3)
            step(v.tensor_copy(iota[:, :], iota_i[:, :]))
            step(v.tensor_copy(part[:, 0:1], part_i[:, :]))
            step(v.tensor_copy(nbase[:, :], nbase_i[:, :]))
            step(v.tensor_scalar(part[:, 1:2], part[:, 0:1], 1.0, None, ALU.is_ge))
            step(v.tensor_scalar(part[:, 2:3], part[:, 0:1], float(P), None, ALU.mult))
            step(v.tensor_scalar(ident[:, :], iota[:, :], part[:, 0:1], None, ALU.is_equal))
            v.tensor_scalar(tri[:, :], iota[:, :], part[:, 0:1], part[:, 1:2], ALU.is_ge, ALU.mult).then_inc(tri_ready, 1)

            def layer_norm(n):
                for half, (a, z1) in enumerate(HALVES):
                    mean, hh = stats[:, 0, a:z1], h[:, a:z1, :]
                    squares = gathered[:, :, :].rearrange("p j c -> p (j c)")[:, 0:(z1 - a) * FEAT].rearrange(
                        "p (k f) -> p k f", f=FEAT)
                    step(v.tensor_reduce(mean, xs[:, a:z1, :], AX.X, ALU.add))
                    step(v.tensor_scalar(mean, mean, 1.0 / FEAT, None, ALU.mult))
                    step(v.tensor_tensor(hh, xs[:, a:z1, :], mean.unsqueeze(2).to_broadcast([P, z1 - a, FEAT]), ALU.subtract))
                    step(v.tensor_tensor(squares, hh, hh, ALU.mult))
                    v.tensor_reduce(stats[:, 1, a:z1], squares, AX.X, ALU.add).then_inc(var_ready, 1)
                    dve.wait_ge(std_ready, 2 * n + half + 1)
                    step(v.reciprocal(stats[:, 3, a:z1], stats[:, 2, a:z1]))
                    v.scalar_tensor_tensor(out=hh, in0=hh, scalar=0.0,
                                           in1=stats[:, 3, a:z1].unsqueeze(2).to_broadcast([P, z1 - a, FEAT]),
                                           op0=ALU.max, op1=ALU.mult).then_inc(h_ready, 1)

            dve.wait_ge(x_loaded, 32)
            layer_norm(0)

            dve.wait_ge(dst_loaded, 48)
            v.tensor_tensor(is_first, dst_now, dst_before, ALU.not_equal).then_inc(flags_ready, 1)
            dve.wait_ge(flags_ready, 1)
            v.tensor_tensor(first_dst[:, :], is_first, dst_now, ALU.mult).then_inc(flags_ready, 1)
            dve.wait_ge(flags_ready, 2)
            dve.wait_ge(last_loaded, 16)
            dve.wait_ge(rel_turned, 2 * len(chunks))
            step(v.tensor_scalar(is_last_below, last_dst, part[0:NT, 2:3], None, ALU.is_lt))
            step(v.tensor_reduce(small[0:NT, 1:2], is_last_below, AX.X, ALU.add))
            step(v.tensor_scalar(small[0:NT, 1:2], small[0:NT, 1:2], float(TILES - 1), None, ALU.min))
            v.tensor_copy(small_i[0:NT, 0:1], small[0:NT, 1:2]).then_inc(at_ready, 1)
            step(v.memset(ones_row, 1.0))
            dve.wait_ge(steps_ready, len(chunks))
            v.tensor_tensor_scan(base_row, ones_row, steps_row, -1.0, ALU.mult, ALU.add).then_inc(base_ready, 1)
            dve.wait_ge(base_ready, 1)
            v.tensor_copy(base_regs.rearrange("o (g e) -> o g e", e=8)[:, :, 0:GROUP],
                          base_row.rearrange("o (g e) -> o g e", e=GROUP)).then_inc(regs_ready, 1)
            dve.wait_ge(at_gathered, 32)
            step(v.tensor_scalar(below, dst_at, part[0:NT, 2:3], None, ALU.is_lt))
            step(v.tensor_tensor(differs[:, 1:P], dst_at[:, 1:P], dst_at[:, 0:P - 1], ALU.not_equal))
            step(v.memset(differs[:, 0:1], 1.0))
            step(v.tensor_tensor(below, below, differs, ALU.mult))
            step(v.tensor_reduce(small[0:NT, 2:3], below, AX.X, ALU.add))
            step(v.tensor_tensor(small[0:NT, 3:4], small[0:NT, 2:3], small[0:NT, 0:1], ALU.add))
            v.tensor_copy(small_i[0:NT, 1:2], small[0:NT, 3:4]).then_inc(first_ready, 1)
            dve.wait_ge(first_ready, 1)
            dve.wait_ge(src_loaded, 32)
            v.tensor_copy(idx[:, :], src[:, 0:BODY]).then_inc(idx_ready, GROUPS_IN_BODY)

            def next_indices(t, q):
                v.tensor_copy(idx[:, q * GROUP:(q + 1) * GROUP],
                              src[:, bass.ds(t + BODY, GROUP)]).then_inc(idx_ready, 1)

            def make_pick(g, s, j):
                v.tensor_scalar(pick[:, s, j, :], iota[:, :], rel[:, bass.ds(g * GROUP + j, 1)], None,
                                ALU.is_equal).then_inc(pick_ready, 1)

            def load_bases(g):
                _, ranks = nc.values_load_multi_w_load_instructions(
                    base_regs[:, bass.ds(g * 8, GROUP)], engines=[DVE_ENGINE],
                    min_val=0, max_val=RANKS - P,
                    skip_runtime_bounds_check_because="ranks are below the number of nodes")
                return ranks

            def add_sums(n0, ranks, rows, ps_sum, between):
                dve.wait_ge(sums_ready, n0 + (CREDIT + GROUP))
                for j in range(GROUP):
                    dve.wait_ge(sums_added, n0 + (CREDIT + j))
                    to = acc[0:rows, bass.ds(ranks[j], P)]
                    v.tensor_tensor(to, to, ps_sum[0:rows, j, :], ALU.add).then_inc(sums_added, 1)
                    between(j)

            def stage_batch(b):
                _, ranks = nc.values_load_multi_w_load_instructions(
                    first_rank_regs[:, bass.ds(b * 8, BATCH)], engines=[DVE_ENGINE],
                    min_val=0, max_val=RANKS - P,
                    skip_runtime_bounds_check_because="ranks are at most the number of nodes")
                for m in range(BATCH):
                    ins = v.tensor_copy(stage[0:FEAT + 1, m, :], acc[0:FEAT + 1, bass.ds(ranks[m], P)])
                ins.then_inc(staged, 1)

            def make_spread(n, b):
                dve.wait_ge(turn_copied, n + 1)
                for m in range(BATCH):
                    ins = v.tensor_scalar(spread[:, m, :], iota[:, :], nbase[:, bass.ds(b * BATCH + m, 1)],
                                          turned[:, m, FEAT:FEAT + 1], ALU.add, ALU.is_equal)
                ins.then_inc(spread_ready, 1)

            dve.wait_ge(rel_copied, len(chunks))
            dve.wait_ge(first_loaded, 16)
            with dve.Fori(0, HOPS) as hop:
                v.memset(acc[0:FEAT + 1, :], 0.0).then_inc(acc_zero, 1)
                dve.wait_ge(acc_zero, hop + 1)
                dve.sem_inc(dve_passed, 1)
                with dve.Fori(0, ROUNDS) as i:
                    for q in range(GROUPS_IN_BODY):
                        g = i * GROUPS_IN_BODY + q
                        for j in range(GROUP):
                            make_pick(g, 0, j)
                        add_sums(hop * TILES + g * GROUP, load_bases(g), FEAT + 1, ps_sums[0], lambda j: None)
                        next_indices(g * GROUP, q)
                with dve.Fori(0, NBATCH) as b:
                    n = hop * NBATCH + b
                    dve.wait_ge(sums_added, (hop + 1) * TILES + CREDIT)
                    stage_batch(b)
                    make_spread(n, b)
                dve.wait_ge(staged, (hop + 1) * NBATCH)

            step(v.memset(acc[0:FEAT, :], 0.0))
            dve.wait_ge(table_ready, 16 * NBATCH * (HOPS + 1))
            step(v.tensor_tensor(xs[:, :, :], xs[:, :, :], h[:, :, :], ALU.add))
            layer_norm(1)
            dve.wait_ge(h_ready, 4)
            v.memset(turned[FEAT:FEAT + 1, :, :], 1.0).then_inc(residual_done, 1)
            dve.wait_ge(node_loaded, 16)
            step(v.tensor_copy(node_i[:, :], node_f[:, :]))

            def keep_products(n):
                dve.wait_ge(p_done, n + 1)
                dve.wait_ge(p_stored, n * 16 + 16 * CREDIT)
                v.tensor_copy(rows_out, ps_b).then_inc(p_kept, 1)

            def keep_parts(n):
                dve.wait_ge(p_done, n + 1)
                dve.wait_ge(p_stored, n * 16 + 16 * CREDIT)
                k = (n - NBATCH) * 4
                v.tensor_copy(parts_out[:, :, 0, :], ps_b).then_inc(split_steps, 1)
                dve.wait_ge(split_steps, k + 1)
                v.tensor_tensor(rest, ps_b, parts_out[:, :, 0, :], ALU.subtract).then_inc(split_steps, 1)
                dve.wait_ge(split_steps, k + 2)
                v.tensor_copy(parts_out[:, :, 1, :], rest).then_inc(split_steps, 1)
                dve.wait_ge(split_steps, k + 3)
                v.tensor_tensor(parts_out[:, :, 2, :], rest, parts_out[:, :, 1, :], ALU.subtract).then_inc(split_steps, 1)
                dve.wait_ge(split_steps, k + 4)
                dve.sem_inc(p_kept, 1)

            with dve.Fori(0, NBATCH) as b:
                keep_products(b)
            with dve.Fori(0, RBATCH) as b:
                dve.wait_ge(node_used, b + CREDIT)
                v.tensor_copy(node_idx[:, :], node_i[:, bass.ds(b * BATCH, BATCH)]).then_inc(node_idx_ready, 1)
                keep_parts(b + NBATCH)
            dve.wait_ge(p_stored, 16 * (CREDIT + NBATCH + RBATCH))

            def edge_sum(i, o):
                g, q = i * CONV_BODY + o, o % GROUPS_IN_BODY
                dve.wait_ge(z_done, g + (CREDIT + 1))
                for j in range(GROUP):
                    dve.wait_ge(gather_done[q * GROUP + j],
                                i * (16 * CONV_BODY // GROUPS_IN_BODY) + 16 * (o // GROUPS_IN_BODY + HOPS * ROUNDS + 1))
                v.tensor_tensor(z, ps_z, gathered[:, q * GROUP:(q + 1) * GROUP, :], ALU.add).then_inc(z_ready, 1)
                dve.wait_ge(z_ready, g + 1)
                dve.sem_inc(slot_free, GROUP)
                dve.sem_inc(z_read, 1)

            def log_sums(g):
                dve.wait_ge(logs_ready, g + 1)
                v.scalar_tensor_tensor(out=lg[:, :, 0:FEAT], in0=z[:, :, 0:FEAT], scalar=0.0, in1=lg[:, :, 0:FEAT],
                                       op0=ALU.min, op1=ALU.subtract).then_inc(gate_arg, 1)
                v.scalar_tensor_tensor(out=lg[:, :, FEAT:F2], in0=z[:, :, FEAT:F2], scalar=0.0, in1=lg[:, :, FEAT:F2],
                                       op0=ALU.max, op1=ALU.add).then_inc(soft_ready, 1)
                dve.wait_ge(gate_arg, g + 1)
                dve.wait_ge(soft_ready, g + 1)

            def messages(g, s):
                dve.wait_ge(gate_ready, g + 1)
                v.tensor_tensor(msg[:, s, :, 0:FEAT], lg[:, :, 0:FEAT], lg[:, :, FEAT:F2], ALU.mult).then_inc(msg_ready, 1)

            def add_group(g, o, between):
                add_sums(g * GROUP + HOPS * TILES, load_bases(g), FEAT, ps_sums[o % 2], between)

            def conv_step(i, o):
                looped = not isinstance(i, int)
                g = i * CONV_BODY + o
                log_sums(g)
                if looped or g + 1 < GROUPS:
                    edge_sum(i, o + 1)
                messages(g, o % 2)
                if looped or g + GROUPS_IN_BODY < GROUPS:
                    next_indices(g * GROUP, o % GROUPS_IN_BODY)

                def ahead(j):
                    if looped or g + 3 < GROUPS:
                        make_pick(g + 3, (o + 3) % GROUPS_IN_BODY, j)

                if looped or g:
                    add_group(g - 1, o - 1, ahead)
                else:
                    for j in range(GROUP):
                        ahead(j)

            for g in range(3):
                for j in range(GROUP):
                    make_pick(g, g, j)
            edge_sum(0, 0)
            conv_step(0, 0)
            with dve.Fori(0, CONV_ROUNDS) as i:
                for o in range(1, CONV_BODY + 1):
                    conv_step(i, o)
            for o in TAIL:
                conv_step(CONV_ROUNDS, o)
            add_group(GROUPS - 1, GROUPS - 1, lambda j: None)

            dve.wait_ge(sums_added, (HOPS + 1) * TILES + CREDIT)
            with dve.Fori(0, NBATCH) as b:
                n = b + HOPS * NBATCH
                stage_batch(b)
                make_spread(n, b)
                dve.wait_ge(batch_done, n + 1)
                to = h[:, bass.ds(b * BATCH, BATCH), :]
                v.tensor_tensor(to, to, ps_b[:, :, 0:FEAT], ALU.add).then_inc(batch_kept, 1)
            dve.wait_ge(batch_kept, (HOPS + 1) * NBATCH)
            v.memset(turned[FEAT:FEAT + 1, :, :], 1.0).then_inc(residual_done, 1)
            with dve.Fori(0, NBATCH) as b:
                n = b + (NBATCH + RBATCH)
                dve.wait_ge(p_done, n + 1)
                dve.wait_ge(out_stored, b * 16 + 16 * CREDIT)
                v.scalar_tensor_tensor(out=rows_out[:, :, 0:FEAT], in0=ps_b[:, :, 0:FEAT], scalar=0.0,
                                       in1=xs[:, bass.ds(b * BATCH, BATCH), :],
                                       op0=ALU.max, op1=ALU.add).then_inc(f_kept, 1)
                dve.wait_ge(f_kept, b + (CREDIT + 1))
                dve.sem_inc(p_kept, 1)


def kernel(x, src, dst, edge_attr_32, edge_weight, L1_gnn_Wf, L1_gnn_bf, L1_gnn_Ws, L1_gnn_bs, L1_gnn_Wm, L1_gnn_bm):
    import numpy as np
    import concourse.bacc as bacc
    from concourse.bass_utils import run_bass_kernel_spmd

    def cols(a):
        return np.ascontiguousarray(np.asarray(a).reshape(-1, P).T)

    arrays = {
        "x": np.ascontiguousarray(x),
        "src_t": cols(src),
        "dst_t": cols(dst),
        "dst_rows": np.ascontiguousarray(np.asarray(dst).reshape(-1, P)),
        "w_t": cols(edge_weight),
        "attr_t": np.ascontiguousarray(np.asarray(edge_attr_32).T),
        "w_f": np.ascontiguousarray(L1_gnn_Wf),
        "w_s": np.ascontiguousarray(L1_gnn_Ws),
        "b_f": np.ascontiguousarray(L1_gnn_bf).reshape(1, -1),
        "b_s": np.ascontiguousarray(L1_gnn_bs).reshape(1, -1),
        "w_m": np.ascontiguousarray(L1_gnn_Wm),
        "b_m": np.ascontiguousarray(L1_gnn_bm).reshape(1, -1),
    }
    nc = bacc.Bacc("TRN2", target_bir_lowering=False, num_devices=1)
    args = [nc.dram_tensor(name, a.shape, mybir.dt.from_np(a.dtype), kind="ExternalInput").ap()
            for name, a in arrays.items()]
    out = nc.dram_tensor("out", arrays["x"].shape, F32, kind="ExternalOutput").ap()
    build(nc, *args, out)
    r = run_bass_kernel_spmd(nc, [arrays], core_ids=[0])
    return r.results[0]["out"]
```

```python
from contextlib import ExitStack

import concourse.bass as bass
from concourse import mybir

P = 128
F32 = mybir.dt.float32
BF16 = mybir.dt.bfloat16
I32 = mybir.dt.int32
ALU = mybir.AluOpType
ACT = mybir.ActivationFunctionType
AX = mybir.AxisListType
DVE_ENGINE = mybir.EngineType.DVE
SP_ENGINE = mybir.EngineType.SP
POOL_ENGINE = mybir.EngineType.Pool
ACT_ENGINE = mybir.EngineType.Activation

HOPS = 3
GROUP = 5
GROUPS_IN_BODY = 5
SLOTS = 3
CONV_BODY = 10
BATCH = 7
BY_ACT = 3
EPS = 1e-5


def build(nc, x, src_t, dst_t, dst_rows, w_t, attr_t, w_f, w_s, b_f, b_s, w_m, b_m, out):
    NODES, FEAT = x.shape
    TILES = src_t.shape[1]
    EDIM = attr_t.shape[0]
    BODY = GROUP * GROUPS_IN_BODY
    ROUNDS = TILES // BODY
    GROUPS = TILES // GROUP
    NT = -(-NODES // P)
    NT_FULL = NODES // P
    NREST = NODES - NT_FULL * P
    NBATCH = NT // BATCH
    RT = -(-(NODES + P) // (P * BATCH)) * BATCH
    RBATCH = RT // BATCH
    RANKS = RT * P
    F2 = 2 * FEAT
    HALVES = [(0, NT // 2), (NT // 2, NT)]
    chunks = [(a, min(a + 512, TILES)) for a in range(0, TILES, 512)]
    assert dst_t.shape[0] == P and TILES % BODY == 0 and NT % BATCH == 0 and FEAT == 64

    CREDIT = BODY

    CONV_ROUNDS = (GROUPS - 1) // CONV_BODY
    TAIL = range(1, GROUPS - CONV_ROUNDS * CONV_BODY)
    assert CONV_BODY % GROUPS_IN_BODY == 0 and CONV_BODY % 2 == 0

    ctx = ExitStack()
    with ctx:
        def sb(name, shape, dt=F32):
            return ctx.enter_context(nc.sbuf_tensor(name, shape, dt))

        def sem(name):
            return ctx.enter_context(nc.semaphore(name))

        def dram(name, shape, dt=F32):
            return nc.dram_tensor(name, shape, dt, kind="Internal").ap()

        h_table = dram("h_table", (NT * P, FEAT))
        src_table = dram("src_table", (NT * P, F2))
        dst_by_rank = dram("dst_by_rank", (RANKS, 3 * F2), BF16)
        base_dram = dram("base_dram", (TILES, 1))
        first_rank_dram = dram("first_rank_dram", (NT, 1), I32)
        node_dram = dram("node_dram", (RANKS, 1))

        acc = sb("acc", [P, RANKS])
        xs = sb("xs", [P, NT, FEAT])
        h = sb("h", [P, NT, FEAT])
        src = sb("src", [P, TILES + BODY], I32)
        w = sb("w", [P, TILES])
        rel = sb("rel", [P, TILES])
        first_dst = sb("first_dst", [P, TILES])
        gathered = sb("gathered", [P, BODY, F2])
        idx = sb("idx", [P, BODY], I32)
        msg = sb("msg", [P, SLOTS, GROUP, FEAT + 1])
        pick = sb("pick", [P, GROUPS_IN_BODY, GROUP, P])
        iota = sb("iota", [P, P])
        part = sb("part", [P, 4])
        nbase = sb("nbase", [P, NT])
        ident = sb("ident", [P, P])
        tri = sb("tri", [P, P])
        stats = sb("stats", [P, 4, NT])
        eps = sb("eps", [P, 1])
        small = sb("small", [P, 8])
        small_i = sb("small_i", [P, 2], I32)
        node_f = sb("node_f", [P, RT])
        node_i = sb("node_i", [P, RT], I32)
        node_idx = sb("node_idx", [P, 2, BATCH], I32)
        w_src = sb("w_src", [FEAT, F2])
        w_dst = sb("w_dst", [FEAT + 1, F2])
        w_edge = sb("w_edge", [EDIM, F2])
        w_out = sb("w_out", [FEAT + 1, FEAT])

        BP = BATCH * P
        scratch = sb("scratch", [P, 4 * BP])
        flat = gathered[:, :, :].rearrange("p j c -> p (j c)")

        def batch_of(memory, n):
            return memory[:, n * BP:(n + 1) * BP].rearrange("p (m c) -> p m c", m=BATCH)

        turned = [batch_of(scratch, 0), batch_of(scratch, 1)]
        spread = [batch_of(scratch, 3), batch_of(flat, 2)]
        stage = [batch_of(flat, 0), batch_of(flat, 1)]
        rows_out = [batch_of(scratch, 2), batch_of(scratch, 3)]
        p_stage = batch_of(scratch, 3)
        squares = [flat[:, 0:(NT // 2) * FEAT].rearrange("p (k f) -> p k f", f=FEAT),
                   scratch[:, 0:(NT // 2) * FEAT].rearrange("p (k f) -> p k f", f=FEAT)]
        node_rows_at = first_dst[:, 0:2 * BATCH * FEAT].rearrange("p (s m f) -> p s m f", s=2, m=BATCH)
        parts_out = first_dst[:, 2 * BATCH * FEAT:2 * BATCH * FEAT + 3 * BP // 2].bitcast(BF16).rearrange(
            "p (m n c) -> p m n c", m=BATCH, n=3)
        Q_WIN = 2 * GROUP * 3 * F2 // 2
        rest = w[:, Q_WIN:Q_WIN + BP].rearrange("p (m c) -> p m c", m=BATCH)
        G1 = GROUP * P
        in_group = scratch[:, 0:4 * G1].rearrange("p (n j c) -> p n j c", n=4, j=GROUP)
        zs, e, lg = [in_group[:, 0], in_group[:, 1]], in_group[:, 2], in_group[:, 3]
        pick_t = scratch[:, 4 * G1:4 * G1 + G1 // 2].bitcast(BF16).rearrange("p (j c) -> p j c", j=GROUP)
        iota_i = scratch[:, 0:P].bitcast(I32)
        nbase_i = scratch[:, P:P + NT].bitcast(I32)
        part_i = scratch[:, 2 * P:2 * P + 1].bitcast(I32)
        q_win = w[:, 0:Q_WIN].bitcast(BF16).rearrange("p (s j c) -> p s j c", s=2, j=GROUP)
        attr = sb("attr", [EDIM, 2, GROUP * P])

        psum = ctx.enter_context(nc.psum_tensor("psum", [P, 8 * 512], F32))
        ps_sums = [psum[:, a:a + G1].rearrange("p (j c) -> p j c", j=GROUP) for a in (0, 1024, 2048)]
        ps_turn = psum[:, 2048:2048 + G1].rearrange("p (j c) -> p j c", j=GROUP)
        ps_z = psum[:, 3072:3072 + G1].rearrange("p (j c) -> p j c", j=GROUP)
        ps_a = [psum[:, a:a + BP].rearrange("p (m c) -> p m c", m=BATCH) for a in (0, 1024)]
        ps_b = [psum[:, a:a + BP].rearrange("p (m c) -> p m c", m=BATCH) for a in (2048, 3072)]

        dst_now = acc[:, 0:TILES].bitcast(I32)
        dst_before = acc[:, TILES:2 * TILES].bitcast(I32)
        is_first = acc[:, 2 * TILES:3 * TILES]
        last_dst = acc[0:NT, 3 * TILES:4 * TILES].bitcast(I32)
        ROW = 96
        steps_row = acc[ROW:ROW + 1, 0:TILES]
        ones_row = acc[ROW:ROW + 1, TILES:2 * TILES]
        base_row = acc[ROW:ROW + 1, 2 * TILES:3 * TILES]
        base_regs = acc[ROW:ROW + 1, 0:8 * GROUPS].bitcast(I32)
        first_rank_regs = acc[ROW:ROW + 1, 8 * GROUPS:8 * GROUPS + 8 * NBATCH].bitcast(I32)
        dst_at = scratch[0:NT, 0:P].bitcast(I32)
        below = scratch[0:NT, P:2 * P]
        differs = scratch[0:NT, 2 * P:3 * P]
        is_last_below = acc[0:NT, 2 * TILES:3 * TILES]

        pool_passed = sem("pool_passed")
        pe_passed = sem("pe_passed")
        dve_passed = sem("dve_passed")
        act_passed = sem("act_passed")
        consts_made = sem("consts_made")
        x_half = [sem(f"x_half_{n}") for n in range(2)]
        dst_loaded = sem("dst_loaded")
        last_loaded = sem("last_loaded")
        src_loaded = sem("src_loaded")
        w_loaded = sem("w_loaded")
        weights_loaded = sem("weights_loaded")
        dve_chain = sem("dve_chain")
        tail_zeroed = sem("tail_zeroed")
        var_ready = sem("var_ready")
        std_ready = sem("std_ready")
        h_ready = sem("h_ready")
        table_ready = sem("table_ready")
        tri_ready = sem("tri_ready")
        flags_ready = sem("flags_ready")
        rel_turned = sem("rel_turned")
        rel_copied = sem("rel_copied")
        steps_ready = sem("steps_ready")
        base_ready = sem("base_ready")
        base_stored = sem("base_stored")
        at_ready = sem("at_ready")
        at_gathered = sem("at_gathered")
        first_ready = sem("first_ready")
        first_stored = sem("first_stored")
        first_loaded = sem("first_loaded")
        regs_ready = sem("regs_ready")
        idx_ready = sem("idx_ready")
        gather_done = [sem(f"gather_done_{j}") for j in range(BODY)]
        slot_free = sem("slot_free")
        pick_ready = sem("pick_ready")
        sums_ready = sem("sums_ready")
        sums_added = sem("sums_added")
        staged_by_pool = sem("staged_by_pool")
        staged_by_act = sem("staged_by_act")
        acc_zero = sem("acc_zero")
        turn_done = sem("turn_done")
        turn_copied = sem("turn_copied")
        spread_ready = sem("spread_ready")
        batch_done = sem("batch_done")
        batch_kept = sem("batch_kept")
        residual_done = sem("residual_done")
        node_stored = sem("node_stored")
        node_loaded = sem("node_loaded")
        nodes_ready = sem("nodes_ready")
        node_idx_ready = sem("node_idx_ready")
        node_rows = [[sem(f"node_rows_{s}_{m}") for m in range(BATCH)] for s in range(2)]
        squares_ready = sem("squares_ready")
        centred = sem("centred")
        x_added = sem("x_added")
        q_turned = sem("q_turned")
        q_copied = sem("q_copied")
        q_done = sem("q_done")
        q_kept = sem("q_kept")
        q_stored = sem("q_stored")
        f_staged = sem("f_staged")
        f_turned = sem("f_turned")
        f_copied = sem("f_copied")
        f_done = sem("f_done")
        p_staged = sem("p_staged")
        p_turned = sem("p_turned")
        p_copied = sem("p_copied")
        p_done = sem("p_done")
        p_kept = sem("p_kept")
        p_stored = sem("p_stored")
        split_steps = sem("split_steps")
        group_loaded = [sem(f"group_loaded_{s}") for s in range(2)]
        pick_turned = sem("pick_turned")
        pick_t_ready = sem("pick_t_ready")
        z_done = sem("z_done")
        z_ready = sem("z_ready")
        z_read = sem("z_read")
        gate_arg = sem("gate_arg")
        soft_ready = sem("soft_ready")
        logs_ready = sem("logs_ready")
        act_steps = sem("act_steps")
        gate_ready = sem("gate_ready")
        msg_ready = sem("msg_ready")
        f_kept = sem("f_kept")
        out_stored = [sem(f"out_stored_{s}") for s in range(2)]

        h_table_v = h_table.rearrange("(k p) f -> p k f", p=P)
        src_table_v = src_table.rearrange("(k p) f -> p k f", p=P)
        rank_v = dst_by_rank.rearrange("(p j) (n f) -> p j n f", p=P, n=3)

        block = ctx.enter_context(nc.Block())

        def batches(eng, stages, base=0):
            peeled = len(stages) // 2 * 2

            def step(k, o, looped):
                for d, stage_of in enumerate(stages):
                    if looped or 0 <= k - d < NBATCH:
                        stage_of(base + k - d, k - d, (o - d) % 2)

            for k in range(peeled):
                step(k, k, False)
            with eng.Fori(0, (NBATCH - peeled) // 2) as b:
                for s in range(2):
                    step(b * 2 + (peeled + s), s, True)
            for k in range(NBATCH, NBATCH + len(stages) - 1):
                step(k, k, False)

        def window_ranks(eng, k, some):
            _, ranks = nc.values_load_multi_w_load_instructions(
                first_rank_regs[:, bass.ds(k * 8 + some[0], len(some))], engines=[eng],
                min_val=0, max_val=RANKS - P,
                skip_runtime_bounds_check_because="ranks are at most the number of nodes")
            return zip(some, ranks)

        @block.sync
        def _(sp):
            sp.wait_ge(tail_zeroed, 1)
            for n, (a, z1) in enumerate(HALVES):
                z1 = min(z1, NT_FULL)
                sp.dma_start(xs[:, a:z1, :], x[a * P:z1 * P].rearrange("(k p) f -> p k f", p=P)).then_inc(x_half[n], 16)
            sp.dma_start(xs[0:NREST, NT_FULL, :], x[NT_FULL * P:NODES]).then_inc(x_half[1], 16)
            sp.dma_start(src[:, 0:TILES], src_t).then_inc(src_loaded, 16)
            sp.dma_start(src[:, TILES:TILES + BODY], src_t[:, 0:BODY]).then_inc(src_loaded, 16)
            sp.dma_start(w[:, :], w_t).then_inc(w_loaded, 16)
            for dst_ap, a in ((w_dst[0:FEAT], (0, FEAT)), (w_src[:], (FEAT, F2)), (w_edge[:], (F2, F2 + EDIM))):
                sp.dma_start(dst_ap[:, 0:FEAT], w_f[a[0]:a[1]]).then_inc(weights_loaded, 16)
                sp.dma_start(dst_ap[:, FEAT:F2], w_s[a[0]:a[1]]).then_inc(weights_loaded, 16)
            sp.dma_start(w_dst[FEAT:FEAT + 1, 0:FEAT], b_f).then_inc(weights_loaded, 16)
            sp.dma_start(w_dst[FEAT:FEAT + 1, FEAT:F2], b_s).then_inc(weights_loaded, 16)
            sp.dma_start(w_out[0:FEAT, :], w_m).then_inc(weights_loaded, 16)
            sp.dma_start(w_out[FEAT:FEAT + 1, :], b_m).then_inc(weights_loaded, 16)

            for n, (a, z1) in enumerate(HALVES):
                sp.wait_ge(h_ready, n + 1)
                sp.dma_start(h_table_v[:, a:z1, :], h[:, a:z1, :]).then_inc(table_ready, 8 * NBATCH)

            sp.wait_ge(base_ready, 1)
            sp.dma_start(base_dram.rearrange("t o -> o t"), base_row).then_inc(base_stored, 16)
            sp.wait_ge(first_ready, 1)
            sp.dma_start(first_rank_dram, small_i[0:NT, 1:2]).then_inc(first_stored, 16)
            sp.wait_ge(first_stored, 16)
            sp.wait_ge(regs_ready, 1)
            sp.dma_start(first_rank_regs.rearrange("o (b e) -> o b e", e=8)[:, :, 0:BATCH],
                         first_rank_dram.rearrange("(b e) o -> o b e", e=BATCH)).then_inc(first_loaded, 16)

            with sp.Fori(0, HOPS) as hop:
                with sp.Fori(0, NBATCH) as b:
                    sp.wait_ge(batch_kept, hop * NBATCH + b + (CREDIT + 1))
                    sp.dma_start(h_table_v[:, bass.ds(b * BATCH, BATCH), :],
                                 h[:, bass.ds(b * BATCH, BATCH), :]).then_inc(table_ready, 16)

            sp.wait_ge(batch_kept, CREDIT + HOPS * NBATCH)
            sp.dma_start(node_dram.rearrange("r o -> o r"), acc[FEAT:FEAT + 1, :]).then_inc(node_stored, 16)
            sp.wait_ge(node_stored, 16)
            sp.dma_start(node_f[:, :], node_dram.rearrange("(p j) o -> p (j o)", p=P)).then_inc(node_loaded, 16)
            sp.wait_ge(table_ready, 16 * NBATCH * (HOPS + 1))
            for n, (a, z1) in enumerate(HALVES):
                sp.wait_ge(h_ready, n + 3)
                sp.dma_start(h_table_v[:, a:z1, :], h[:, a:z1, :]).then_inc(table_ready, 8 * NBATCH)
            def store_parts(b):
                sp.wait_ge(q_kept, b + (CREDIT + 1))
                sp.dma_start(rank_v[:, bass.ds(b * BATCH, BATCH), :, :], parts_out).then_inc(q_stored, 16)

            with sp.Fori(0, NBATCH) as b:
                sp.wait_ge(p_kept, b + (CREDIT + 1))
                sp.dma_start(src_table_v[:, bass.ds(b * BATCH, BATCH), :], rows_out[0]).then_inc(p_stored, 16)
                store_parts(b)
            for b in range(NBATCH, RBATCH):
                store_parts(b)
            sp.wait_ge(q_stored, 16 * (CREDIT + RBATCH))

            def load_group(g, s):
                _, ranks = nc.values_load_multi_w_load_instructions(
                    base_regs[:, bass.ds(g * 8, GROUP)], engines=[SP_ENGINE], min_val=0, max_val=RANKS - P,
                    skip_runtime_bounds_check_because="ranks are below the number of nodes")
                sp.wait_ge(z_done, g + (CREDIT - 1))
                sp.dma_start(attr[:, s, :], attr_t[:, bass.ds(g * (GROUP * P), GROUP * P)]).then_inc(group_loaded[s], 16)
                for j in range(GROUP):
                    sp.dma_start(q_win[:, s, j, :], dst_by_rank[bass.ds(ranks[j], P), :]).then_inc(group_loaded[s], 16)

            with sp.Fori(0, GROUPS // 2) as i:
                for s in range(2):
                    load_group(i * 2 + s, s)
            if GROUPS % 2:
                load_group(GROUPS - 1, 0)

            def store_result(b, s):
                sp.wait_ge(f_kept, b + (CREDIT + 1))
                sp.dma_start(out[bass.ds(b * BP, BP), :].rearrange("(k p) f -> p k f", p=P),
                             rows_out[s][:, :, 0:FEAT]).then_inc(out_stored[s], 16)

            with sp.Fori(0, NBATCH // 2 - 1) as b:
                for s in range(2):
                    store_result(b * 2 + s, s)
            store_result(NBATCH - 2, 0)
            sp.wait_ge(f_kept, CREDIT + NBATCH)
            last = (NBATCH - 1) * BP
            sp.dma_start(out[last:NT_FULL * P, :].rearrange("(k p) f -> p k f", p=P),
                         rows_out[1][:, 0:BATCH - 1, 0:FEAT]).then_inc(out_stored[1], 16)
            sp.dma_start(out[NT_FULL * P:NODES, :], rows_out[1][0:NREST, BATCH - 1, 0:FEAT]).then_inc(out_stored[1], 16)
            sp.wait_ge(out_stored[0], 16 * (CREDIT + NBATCH // 2))
            sp.wait_ge(out_stored[1], 16 * (CREDIT + NBATCH // 2 + 1))

        @block.gpsimd
        def _(pool):
            nc.gpsimd.iota(iota_i[:, :], pattern=[[1, P]], base=0, channel_multiplier=0).then_inc(consts_made, 1)
            nc.gpsimd.iota(part_i[:, :], pattern=[[0, 1]], base=0, channel_multiplier=1).then_inc(consts_made, 1)
            nc.gpsimd.iota(nbase_i[:, :], pattern=[[P, NT]], base=0, channel_multiplier=0).then_inc(consts_made, 1)

            def gather(out_ap, table, index, done):
                pool.indirect_dma_start(out=out_ap, out_offset=None, in_=table,
                                        in_offset=bass.IndirectOffsetOnAxis(ap=index, axis=0)).then_inc(done, 16)

            def gather_group(phase, i, q, table, width):
                g = (phase * ROUNDS + i) * GROUPS_IN_BODY + q
                pool.wait_ge(idx_ready, g + 1)
                pool.wait_ge(slot_free, g * GROUP + GROUP)
                pool.sem_inc(pool_passed, 1)
                for j in range(GROUP):
                    k = q * GROUP + j
                    gather(gathered[:, k, 0:width], table, idx[:, k:k + 1], gather_done[k])

            def stage_batch(n, k, s):
                windows = window_ranks(POOL_ENGINE, k, range(BY_ACT, BATCH))
                pool.wait_ge(turn_done, n + (CREDIT - 1))
                for m, rank in windows:
                    ins = nc.gpsimd.tensor_copy(stage[s][0:FEAT + 1, m, :], acc[0:FEAT + 1, bass.ds(rank, P)])
                ins.then_inc(staged_by_pool, 1)

            def gather_hop(hop, first_round):
                with pool.Fori(first_round, ROUNDS) as i:
                    for q in range(GROUPS_IN_BODY):
                        gather_group(hop, i, q, h_table, FEAT)
                pool.wait_ge(sums_added, (hop + 1) * TILES + CREDIT)
                pool.wait_ge(first_loaded, 16)
                pool.sem_inc(pool_passed, 1)
                batches(pool, [stage_batch], hop * NBATCH)

            pool.wait_ge(table_ready, 16 * NBATCH)
            for q in range(GROUPS_IN_BODY):
                gather_group(0, 0, q, h_table, FEAT)
            pool.wait_ge(at_ready, 1)
            pool.wait_ge(base_stored, 16)
            gather(dst_at, dst_rows, small_i[0:NT, 0:1], at_gathered)
            gather(small[0:NT, 0:1], base_dram, small_i[0:NT, 0:1], at_gathered)
            gather_hop(0, 1)
            with pool.Fori(1, HOPS) as hop:
                pool.wait_ge(table_ready, (hop + 1) * (16 * NBATCH))
                pool.sem_inc(pool_passed, 1)
                gather_hop(hop, 0)

            pool.wait_ge(batch_kept, CREDIT + HOPS * NBATCH)
            a, z1 = HALVES[1]
            nc.gpsimd.tensor_tensor(xs[:, a:z1, :], xs[:, a:z1, :], h[:, a:z1, :], ALU.add).then_inc(x_added, 1)
            nc.gpsimd.memset(acc[0:FEAT, :], 0.0).then_inc(acc_zero, 1)

            pool.wait_ge(table_ready, 16 * NBATCH * (HOPS + 2))
            pool.wait_ge(nodes_ready, 1)

            def gather_ranks(b, s):
                pool.wait_ge(q_turned, b + (CREDIT - 1))
                nc.gpsimd.tensor_copy(node_idx[:, s, :], node_i[:, bass.ds(b * BATCH, BATCH)]).then_inc(node_idx_ready, 1)
                pool.wait_ge(node_idx_ready, b + 1)
                pool.sem_inc(pool_passed, 1)
                for m in range(BATCH):
                    gather(node_rows_at[:, s, m, :], h_table, node_idx[:, s, m:m + 1], node_rows[s][m])

            with pool.Fori(0, NBATCH // 2) as b:
                for s in range(2):
                    gather_ranks(b * 2 + s, s)
            for b in range(NBATCH, RBATCH):
                gather_ranks(b, b % 2)

            pool.wait_ge(p_stored, 16 * (CREDIT + NBATCH))
            with pool.Fori(0, ROUNDS) as i:
                for q in range(GROUPS_IN_BODY):
                    gather_group(HOPS, i, q, src_table, F2)
            pool.wait_ge(sums_added, (HOPS + 1) * TILES + CREDIT)
            batches(pool, [stage_batch], HOPS * NBATCH)

            def stage_rows(n, k, s):
                pool.wait_ge(f_turned, n + (CREDIT - 1))
                nc.gpsimd.tensor_copy(stage[s][:, :, 0:FEAT], h[:, bass.ds(n * BATCH, BATCH), :]).then_inc(f_staged, 1)

            pool.wait_ge(batch_kept, CREDIT + (HOPS + 1) * NBATCH)
            batches(pool, [stage_rows])

        @block.scalar
        def _(act):
            act.sem_inc(slot_free, CREDIT)
            act.sem_inc(p_stored, 16 * CREDIT)
            act.sem_inc(q_stored, 16 * CREDIT)
            act.sem_inc(out_stored[0], 16 * CREDIT)
            act.sem_inc(out_stored[1], 16 * CREDIT)
            act.dma_start(dst_now, dst_t).then_inc(dst_loaded, 16)
            act.dma_start(dst_before[1:P, :], dst_t[0:P - 1, :]).then_inc(dst_loaded, 16)
            act.dma_start(dst_before[0:1, 1:TILES], dst_t[P - 1:P, 0:TILES - 1]).then_inc(dst_loaded, 16)
            act.dma_start(last_dst, dst_t[P - 1:P, :].to_broadcast([NT, TILES])).then_inc(last_loaded, 16)

            def std(n):
                a, z1 = HALVES[(n - 1) % 2]
                act.wait_ge(centred, n)
                nc.scalar.activation(squares[n % 2][:, 0:z1 - a, :], h[:, a:z1, :], ACT.Square).then_inc(squares_ready, 1)
                act.wait_ge(var_ready, n)
                nc.scalar.activation(stats[:, 2, a:z1], stats[:, 1, a:z1], ACT.Sqrt, bias=eps[:, :],
                                     scale=1.0 / FEAT).then_inc(std_ready, 1)

            std(1)
            std(2)
            for n, (a, z1) in enumerate(chunks):
                act.wait_ge(rel_turned, n + 1)
                nc.scalar.copy(rel[:, a:z1], psum[:, n * 512:n * 512 + z1 - a]).then_inc(rel_copied, 1)
            act.wait_ge(flags_ready, 2)
            for n, (a, z1) in enumerate(chunks):
                act.wait_ge(rel_turned, len(chunks) + n + 1)
                nc.scalar.copy(steps_row[:, a:z1], psum[0:1, n * 512:n * 512 + z1 - a]).then_inc(steps_ready, 1)

            def scale_group(phase, i, q):
                r = phase * ROUNDS + i
                g = r * GROUPS_IN_BODY + q
                t = i * BODY + q * GROUP
                act.wait_ge(sums_ready, g * GROUP + (CREDIT - GROUP))
                nc.scalar.copy(msg[:, q % SLOTS, :, FEAT], first_dst[:, bass.ds(t, GROUP)])
                for j in range(GROUP):
                    k = q * GROUP + j
                    act.wait_ge(gather_done[k], r * 16 + 16)
                    nc.scalar.activation(msg[:, q % SLOTS, j, 0:FEAT], gathered[:, k, 0:FEAT], ACT.Copy,
                                         scale=w[:, bass.ds(t + j, 1)]).then_inc(slot_free, 1)

            def stage_batch(n, k, s):
                windows = window_ranks(ACT_ENGINE, k, range(BY_ACT))
                act.wait_ge(turn_done, n + (CREDIT - 1))
                for m, rank in windows:
                    ins = nc.scalar.copy(stage[s][0:FEAT + 1, m, :], acc[0:FEAT + 1, bass.ds(rank, P)])
                ins.then_inc(staged_by_act, 1)

            def copy_turned(n, k, s):
                act.wait_ge(turn_done, n + (CREDIT + 1))
                nc.scalar.copy(turned[s][:, :, 0:FEAT + 1], ps_a[s][:, :, 0:FEAT + 1]).then_inc(turn_copied, 1)

            def keep_batch(n, k, s):
                act.wait_ge(batch_done, n + (CREDIT + 1))
                nc.scalar.copy(h[:, bass.ds(k * BATCH, BATCH), :], ps_b[s][:, :, 0:FEAT]).then_inc(batch_kept, 1)

            act.wait_ge(w_loaded, 16)
            act.wait_ge(flags_ready, 2)
            with act.Fori(0, HOPS) as hop:
                with act.Fori(0, ROUNDS) as i:
                    for q in range(GROUPS_IN_BODY):
                        scale_group(hop, i, q)
                act.wait_ge(sums_added, (hop + 1) * TILES + CREDIT)
                act.wait_ge(first_loaded, 16)
                act.sem_inc(act_passed, 1)
                batches(act, [stage_batch, copy_turned, keep_batch], hop * NBATCH)

            std(3)
            std(4)

            act.wait_ge(h_ready, 4)
            act.wait_ge(residual_done, 1)

            def copy_node_rows(b):
                act.wait_ge(q_turned, b + (CREDIT + 1))
                nc.scalar.copy(turned[1][0:FEAT, :, :], ps_a[1][0:FEAT, :, :]).then_inc(q_copied, 1)

            with act.Fori(0, NBATCH) as b:
                act.wait_ge(p_turned, b + CREDIT)
                nc.scalar.copy(p_stage[:, :, 0:FEAT], h[:, bass.ds(b * BATCH, BATCH), :]).then_inc(p_staged, 1)
                act.wait_ge(p_turned, b + (CREDIT + 1))
                nc.scalar.copy(turned[0][0:FEAT, :, :], ps_a[0][0:FEAT, :, :]).then_inc(p_copied, 1)
                copy_node_rows(b)
            for b in range(NBATCH, RBATCH):
                copy_node_rows(b)

            def turn_pick(g):
                act.wait_ge(pick_turned, g + 1)
                nc.scalar.copy(pick_t, ps_turn).then_inc(pick_t_ready, 1)

            def gate_of(g):
                act.wait_ge(gate_arg, g + 1)
                nc.scalar.activation(lg[:, :, 0:FEAT], lg[:, :, 0:FEAT], ACT.Exp).then_inc(gate_ready, 1)

            def log_terms(g, s):
                act.wait_ge(z_ready, g + 1)
                nc.scalar.activation(e, zs[s], ACT.Abs).then_inc(act_steps, 1)
                act.wait_ge(act_steps, g * 2 + 1)
                nc.scalar.activation(e, e, ACT.Exp, scale=-1.0).then_inc(act_steps, 1)
                act.wait_ge(act_steps, g * 2 + 2)
                act.wait_ge(msg_ready, g + CREDIT)
                nc.scalar.activation(lg, e, ACT.Ln, bias=1.0).then_inc(logs_ready, 1)

            def conv_step(i, o):
                g = i * CONV_BODY + o
                gate_of(g)
                if not isinstance(i, int) or g + 1 < GROUPS:
                    log_terms(g + 1, (o + 1) % 2)
                if not isinstance(i, int) or g + 3 < GROUPS:
                    turn_pick(g + 3)

            nc.scalar.preload_act_table_set("natural_log_exp_and_others")
            turn_pick(0)
            turn_pick(1)
            log_terms(0, 0)
            turn_pick(2)
            conv_step(0, 0)
            with act.Fori(0, CONV_ROUNDS) as i:
                for o in range(1, CONV_BODY + 1):
                    conv_step(i, o)
            for o in TAIL:
                conv_step(CONV_ROUNDS, o)

            act.wait_ge(sums_added, (HOPS + 1) * TILES + CREDIT)
            batches(act, [stage_batch, copy_turned], HOPS * NBATCH)
            act.wait_ge(residual_done, 2)

            def copy_rows(n, k, s):
                act.wait_ge(f_turned, n + (CREDIT + 1))
                nc.scalar.copy(turned[s][0:FEAT, :, :], ps_a[s][0:FEAT, :, :]).then_inc(f_copied, 1)

            batches(act, [copy_rows])

        @block.tensor
        def _(pe):
            pe.sem_inc(sums_ready, CREDIT)
            pe.sem_inc(p_turned, CREDIT)
            pe.sem_inc(z_done, CREDIT)
            pe.sem_inc(q_turned, CREDIT)
            pe.sem_inc(turn_done, CREDIT)
            pe.sem_inc(batch_done, CREDIT)
            pe.sem_inc(f_turned, CREDIT)
            pe.wait_ge(tri_ready, 1)
            pe.wait_ge(flags_ready, 1)
            for n, (a, z1) in enumerate(chunks):
                pe.matmul(psum[:, n * 512:n * 512 + z1 - a], tri[:, :], is_first[:, a:z1],
                          start=True, stop=True).then_inc(rel_turned, 1)
            for n, (a, z1) in enumerate(chunks):
                pe.wait_ge(rel_copied, n + 1)
                if a == 0:
                    pe.matmul(psum[0:1, 0:1], ident[:, 0:1], is_first[:, 0:1], start=True, stop=True)
                    pe.matmul(psum[0:1, 1:z1], ident[:, 0:1], is_first[:, 1:z1], start=True, stop=False)
                    pe.matmul(psum[0:1, 1:z1], tri[:, P - 1:P], is_first[:, 0:z1 - 1],
                              start=False, stop=True).then_inc(rel_turned, 1)
                else:
                    to = psum[0:1, n * 512:n * 512 + z1 - a]
                    pe.matmul(to, ident[:, 0:1], is_first[:, a:z1], start=True, stop=False)
                    pe.matmul(to, tri[:, P - 1:P], is_first[:, a - 1:z1 - 1],
                              start=False, stop=True).then_inc(rel_turned, 1)

            pe.wait_ge(steps_ready, len(chunks))

            def sum_group(phase, i, q):
                n0 = ((phase * ROUNDS + i) * GROUPS_IN_BODY + q) * GROUP
                pe.wait_ge(sums_added, n0 + (CREDIT - GROUP))
                for j in range(GROUP):
                    pe.wait_ge(slot_free, n0 + (CREDIT + j + 1))
                    pe.wait_ge(pick_ready, n0 + (j + 1))
                    pe.matmul(ps_sums[q % SLOTS][0:FEAT + 1, j, :], msg[:, q % SLOTS, j, :], pick[:, q, j, :],
                              start=True, stop=True).then_inc(sums_ready, 1)

            def turn_batch(n, k, s):
                pe.wait_ge(staged_by_pool, n + 1)
                pe.wait_ge(staged_by_act, n + 1)
                for m in range(BATCH):
                    mm = pe.transpose(ps_a[s][:, m, 0:FEAT + 1], stage[s][0:FEAT + 1, m, :], ident[0:FEAT + 1, 0:FEAT + 1])
                mm.then_inc(turn_done, 1)

            def spread_batch(n, k, s):
                pe.wait_ge(spread_ready, n + 1)
                pe.wait_ge(batch_kept, n + (CREDIT - 1))
                for m in range(BATCH):
                    mm = pe.matmul(ps_b[s][:, m, 0:FEAT], spread[s][:, m, :], turned[s][:, m, 0:FEAT], start=True, stop=True)
                mm.then_inc(batch_done, 1)

            with pe.Fori(0, HOPS) as hop:
                with pe.Fori(0, ROUNDS) as i:
                    for q in range(GROUPS_IN_BODY):
                        sum_group(hop, i, q)
                batches(pe, [turn_batch, spread_batch], hop * NBATCH)

            def turn_nodes(b):
                pe.wait_ge(p_staged, b + 1)
                pe.sem_inc(pe_passed, 1)
                for m in range(BATCH):
                    mm = pe.transpose(ps_a[0][0:FEAT, m, :], p_stage[:, m, 0:FEAT], ident[:, :])
                mm.then_inc(p_turned, 1)

            def turn_ranks(i, s):
                for m in range(BATCH):
                    pe.wait_ge(node_rows[s][m], i * 16 + 16)
                pe.sem_inc(pe_passed, 1)
                for m in range(BATCH):
                    mm = pe.transpose(ps_a[1][0:FEAT, m, :], node_rows_at[:, s, m, :], ident[:, :])
                mm.then_inc(q_turned, 1)

            def project_nodes(b):
                pe.wait_ge(p_copied, b + 1)
                pe.wait_ge(p_kept, b + CREDIT)
                for m in range(BATCH):
                    mm = pe.matmul(ps_b[0][:, m, :], turned[0][0:FEAT, m, :], w_src[:, :], start=True, stop=True)
                mm.then_inc(p_done, 1)

            def project_ranks(b):
                pe.wait_ge(q_copied, b + 1)
                pe.wait_ge(q_kept, b + CREDIT)
                for m in range(BATCH):
                    mm = pe.matmul(ps_b[1][:, m, :], turned[1][0:FEAT + 1, m, :], w_dst[:, :], start=True, stop=True)
                mm.then_inc(q_done, 1)

            pe.wait_ge(weights_loaded, 16 * 10)
            pe.wait_ge(residual_done, 1)
            with pe.Fori(0, NBATCH // 2) as i:
                for s in range(2):
                    turn_nodes(i * 2 + s)
                    turn_ranks(i, s)
                    project_nodes(i * 2 + s)
                    project_ranks(i * 2 + s)
            for b in range(NBATCH, RBATCH):
                turn_ranks(b // 2, b % 2)
                project_ranks(b)
            pe.wait_ge(p_kept, CREDIT + NBATCH)
            pe.wait_ge(q_kept, CREDIT + RBATCH)

            PHASE0 = HOPS * TILES

            def turn_picks(i, o):
                g = i * CONV_BODY + o
                pe.wait_ge(pick_ready, g * GROUP + (PHASE0 + GROUP))
                for j in range(GROUP):
                    mm = pe.transpose(ps_turn[:, j, :], pick[:, o % GROUPS_IN_BODY, j, :], ident[:, :])
                mm.then_inc(pick_turned, 1)

            def edge_products(i, o):
                g, s = i * CONV_BODY + o, o % 2
                pe.wait_ge(pick_t_ready, g + 1)
                pe.wait_ge(group_loaded[s], (i * (CONV_BODY // 2) + (o // 2 + 1)) * (16 * (GROUP + 1)))
                pe.wait_ge(z_read, g + CREDIT)
                for j in range(GROUP):
                    for n in range(3):
                        pe.matmul(ps_z[:, j, :], pick_t[:, j, :], q_win[:, s, j, n * F2:(n + 1) * F2],
                                  start=(n == 0), stop=False)
                    mm = pe.matmul(ps_z[:, j, :], attr[:, s, j * P:(j + 1) * P], w_edge[:, :], start=False, stop=True)
                mm.then_inc(z_done, 1)

            def sum_messages(i, o):
                g, s = i * CONV_BODY + o, o % 2
                pe.wait_ge(msg_ready, g + (CREDIT + 1))
                pe.wait_ge(sums_added, g * GROUP + (PHASE0 + CREDIT - GROUP))
                for j in range(GROUP):
                    pe.matmul(ps_sums[s][0:FEAT, j, :], msg[:, s, j, 0:FEAT], pick[:, o % GROUPS_IN_BODY, j, :],
                              start=True, stop=True).then_inc(sums_ready, 1)

            def conv_step(i, o):
                looped = not isinstance(i, int)
                if looped or i * CONV_BODY + o + 2 < GROUPS:
                    edge_products(i, o + 2)
                sum_messages(i, o)
                if looped or i * CONV_BODY + o + 3 < GROUPS:
                    turn_picks(i, o + 3)

            for g in range(2):
                turn_picks(0, g)
                edge_products(0, g)
            turn_picks(0, 2)
            conv_step(0, 0)
            with pe.Fori(0, CONV_ROUNDS) as i:
                for o in range(1, CONV_BODY + 1):
                    conv_step(i, o)
            for o in TAIL:
                conv_step(CONV_ROUNDS, o)

            batches(pe, [turn_batch, spread_batch], HOPS * NBATCH)

            def turn_rows(n, k, s):
                pe.wait_ge(f_staged, n + 1)
                pe.sem_inc(pe_passed, 1)
                for m in range(BATCH):
                    mm = pe.transpose(ps_a[s][0:FEAT, m, :], stage[s][:, m, 0:FEAT], ident[:, :])
                mm.then_inc(f_turned, 1)

            def last_products(n, k, s):
                pe.wait_ge(f_copied, n + 1)
                pe.wait_ge(f_kept, n + (CREDIT - 1))
                for m in range(BATCH):
                    mm = pe.matmul(ps_b[s][:, m, 0:FEAT], turned[s][0:FEAT + 1, m, :], w_out[:, :], start=True, stop=True)
                mm.then_inc(f_done, 1)

            batches(pe, [turn_rows, last_products])

        @block.vector
        def _(dve):
            v = nc.vector
            count = [0]

            def step(ins):
                count[0] += 1
                ins.then_inc(dve_chain, 1)
                dve.wait_ge(dve_chain, count[0])

            v.memset(xs[:, NT_FULL, :], 0.0).then_inc(tail_zeroed, 1)
            dve.sem_inc(sums_added, CREDIT)
            dve.sem_inc(p_kept, CREDIT)
            dve.sem_inc(q_kept, CREDIT)
            dve.sem_inc(batch_kept, CREDIT)
            dve.sem_inc(z_read, CREDIT)
            dve.sem_inc(msg_ready, CREDIT)
            dve.sem_inc(f_kept, CREDIT)
            step(v.memset(dst_before[0:1, 0:1], -1))
            step(v.memset(eps[:, :], EPS))
            dve.wait_ge(consts_made, 3)
            step(v.tensor_copy(iota[:, :], iota_i[:, :]))
            step(v.tensor_copy(part[:, 0:1], part_i[:, :]))
            step(v.tensor_copy(nbase[:, :], nbase_i[:, :]))
            step(v.tensor_scalar(part[:, 1:2], part[:, 0:1], 1.0, None, ALU.is_ge))
            step(v.tensor_scalar(part[:, 2:3], part[:, 0:1], float(P), None, ALU.mult))
            step(v.tensor_scalar(ident[:, :], iota[:, :], part[:, 0:1], None, ALU.is_equal))
            v.tensor_scalar(tri[:, :], iota[:, :], part[:, 0:1], part[:, 1:2], ALU.is_ge, ALU.mult).then_inc(tri_ready, 1)

            def layer_norm(n):
                for half, (a, z1) in enumerate(HALVES):
                    mean, hh = stats[:, 0, a:z1], h[:, a:z1, :]
                    if n == 0:
                        dve.wait_ge(x_half[half], 16 * (half + 1))
                    elif half == 1:
                        dve.wait_ge(x_added, 1)
                    step(v.tensor_reduce(mean, xs[:, a:z1, :], AX.X, ALU.add))
                    step(v.tensor_scalar(mean, mean, 1.0 / FEAT, None, ALU.mult))
                    v.tensor_tensor(hh, xs[:, a:z1, :], mean.unsqueeze(2).to_broadcast([P, z1 - a, FEAT]),
                                    ALU.subtract).then_inc(centred, 1)
                for half, (a, z1) in enumerate(HALVES):
                    hh = h[:, a:z1, :]
                    dve.wait_ge(squares_ready, 2 * n + half + 1)
                    v.tensor_reduce(stats[:, 1, a:z1], squares[(half + 1) % 2][:, 0:z1 - a, :], AX.X, ALU.add).then_inc(var_ready, 1)
                    dve.wait_ge(std_ready, 2 * n + half + 1)
                    step(v.reciprocal(stats[:, 3, a:z1], stats[:, 2, a:z1]))
                    v.scalar_tensor_tensor(out=hh, in0=hh, scalar=0.0,
                                           in1=stats[:, 3, a:z1].unsqueeze(2).to_broadcast([P, z1 - a, FEAT]),
                                           op0=ALU.max, op1=ALU.mult).then_inc(h_ready, 1)

            layer_norm(0)

            dve.wait_ge(src_loaded, 32)
            v.tensor_copy(idx[:, :], src[:, 0:BODY]).then_inc(idx_ready, GROUPS_IN_BODY)

            dve.wait_ge(dst_loaded, 48)
            v.tensor_tensor(is_first, dst_now, dst_before, ALU.not_equal).then_inc(flags_ready, 1)
            dve.wait_ge(flags_ready, 1)
            v.tensor_tensor(first_dst[:, :], is_first, dst_now, ALU.mult).then_inc(flags_ready, 1)
            dve.wait_ge(flags_ready, 2)
            dve.wait_ge(last_loaded, 16)
            dve.wait_ge(rel_turned, 2 * len(chunks))
            step(v.tensor_scalar(is_last_below, last_dst, part[0:NT, 2:3], None, ALU.is_lt))
            step(v.tensor_reduce(small[0:NT, 1:2], is_last_below, AX.X, ALU.add))
            step(v.tensor_scalar(small[0:NT, 1:2], small[0:NT, 1:2], float(TILES - 1), None, ALU.min))
            v.tensor_copy(small_i[0:NT, 0:1], small[0:NT, 1:2]).then_inc(at_ready, 1)
            step(v.memset(ones_row, 1.0))
            dve.wait_ge(steps_ready, len(chunks))
            v.tensor_tensor_scan(base_row, ones_row, steps_row, -1.0, ALU.mult, ALU.add).then_inc(base_ready, 1)
            dve.wait_ge(base_ready, 1)
            v.tensor_copy(base_regs.rearrange("o (g e) -> o g e", e=8)[:, :, 0:GROUP],
                          base_row.rearrange("o (g e) -> o g e", e=GROUP)).then_inc(regs_ready, 1)
            dve.wait_ge(at_gathered, 32)
            step(v.tensor_scalar(below, dst_at, part[0:NT, 2:3], None, ALU.is_lt))
            step(v.tensor_tensor(differs[:, 1:P], dst_at[:, 1:P], dst_at[:, 0:P - 1], ALU.not_equal))
            step(v.memset(differs[:, 0:1], 1.0))
            step(v.tensor_tensor(below, below, differs, ALU.mult))
            step(v.tensor_reduce(small[0:NT, 2:3], below, AX.X, ALU.add))
            step(v.tensor_tensor(small[0:NT, 3:4], small[0:NT, 2:3], small[0:NT, 0:1], ALU.add))
            v.tensor_copy(small_i[0:NT, 1:2], small[0:NT, 3:4]).then_inc(first_ready, 1)
            dve.wait_ge(first_ready, 1)
            def next_indices(t, q):
                v.tensor_copy(idx[:, q * GROUP:(q + 1) * GROUP],
                              src[:, bass.ds(t + BODY, GROUP)]).then_inc(idx_ready, 1)

            def make_pick(g, s, j):
                v.tensor_scalar(pick[:, s, j, :], iota[:, :], rel[:, bass.ds(g * GROUP + j, 1)], None,
                                ALU.is_equal).then_inc(pick_ready, 1)

            def load_bases(g):
                _, ranks = nc.values_load_multi_w_load_instructions(
                    base_regs[:, bass.ds(g * 8, GROUP)], engines=[DVE_ENGINE],
                    min_val=0, max_val=RANKS - P,
                    skip_runtime_bounds_check_because="ranks are below the number of nodes")
                return ranks

            def add_sums(n0, ranks, rows, ps_sum, between):
                dve.wait_ge(sums_ready, n0 + (CREDIT + GROUP))
                for j in range(GROUP):
                    dve.wait_ge(sums_added, n0 + (CREDIT + j))
                    to = acc[0:rows, bass.ds(ranks[j], P)]
                    v.tensor_tensor(to, to, ps_sum[0:rows, j, :], ALU.add).then_inc(sums_added, 1)
                    between(j)

            def make_spread(n, k, s):
                dve.wait_ge(turn_copied, n + 1)
                dve.wait_ge(batch_done, n + (CREDIT - 1))
                for m in range(BATCH):
                    ins = v.tensor_scalar(spread[s][:, m, :], iota[:, :], nbase[:, bass.ds(k * BATCH + m, 1)],
                                          turned[s][:, m, FEAT:FEAT + 1], ALU.add, ALU.is_equal)
                ins.then_inc(spread_ready, 1)

            def hop_step(hop, i, q):
                g = i * GROUPS_IN_BODY + q

                def ahead(j):
                    if not isinstance(i, int) or g + 1 < GROUPS:
                        make_pick(g + 1, (q + 1) % GROUPS_IN_BODY, j)

                add_sums(hop * TILES + g * GROUP, load_bases(g), FEAT + 1, ps_sums[q % SLOTS], ahead)
                next_indices(g * GROUP, q)

            dve.wait_ge(rel_copied, len(chunks))
            with dve.Fori(0, HOPS) as hop:
                v.memset(acc[0:FEAT + 1, :], 0.0).then_inc(acc_zero, 1)
                dve.wait_ge(acc_zero, hop + 1)
                dve.sem_inc(dve_passed, 1)
                for j in range(GROUP):
                    make_pick(0, 0, j)
                with dve.Fori(0, ROUNDS - 1) as i:
                    for q in range(GROUPS_IN_BODY):
                        hop_step(hop, i, q)
                for q in range(GROUPS_IN_BODY):
                    hop_step(hop, ROUNDS - 1, q)
                batches(dve, [make_spread], hop * NBATCH)
                dve.wait_ge(turn_done, (hop + 1) * NBATCH + CREDIT)

            dve.wait_ge(batch_kept, CREDIT + HOPS * NBATCH)
            a, z1 = HALVES[0]
            step(v.tensor_tensor(xs[:, a:z1, :], xs[:, a:z1, :], h[:, a:z1, :], ALU.add))
            dve.wait_ge(table_ready, 16 * NBATCH * (HOPS + 1))
            layer_norm(1)
            dve.wait_ge(h_ready, 4)
            step(v.memset(turned[0][FEAT:FEAT + 1, :, :], 1.0))
            v.memset(turned[1][FEAT:FEAT + 1, :, :], 1.0).then_inc(residual_done, 1)
            dve.wait_ge(node_loaded, 16)
            v.tensor_copy(node_i[:, :], node_f[:, :]).then_inc(nodes_ready, 1)

            def keep_products(b):
                dve.wait_ge(p_done, b + 1)
                dve.wait_ge(p_stored, b * 16 + 16 * CREDIT)
                v.tensor_copy(rows_out[0], ps_b[0]).then_inc(p_kept, 1)

            def keep_parts(b):
                dve.wait_ge(q_done, b + 1)
                dve.wait_ge(q_stored, b * 16 + 16 * CREDIT)
                k = b * 3
                v.tensor_copy(parts_out[:, :, 0, :], ps_b[1]).then_inc(split_steps, 1)
                dve.wait_ge(split_steps, k + 1)
                v.tensor_tensor(rest, ps_b[1], parts_out[:, :, 0, :], ALU.subtract).then_inc(split_steps, 1)
                dve.wait_ge(split_steps, k + 2)
                v.tensor_copy(parts_out[:, :, 1, :], rest).then_inc(split_steps, 1)
                dve.wait_ge(split_steps, k + 3)
                v.tensor_tensor(parts_out[:, :, 2, :], rest, parts_out[:, :, 1, :], ALU.subtract).then_inc(q_kept, 1)

            with dve.Fori(0, NBATCH // 2) as i:
                for s in range(2):
                    keep_products(i * 2 + s)
                    keep_parts(i * 2 + s)
            for b in range(NBATCH, RBATCH):
                keep_parts(b)
            dve.wait_ge(p_stored, 16 * (CREDIT + NBATCH))
            dve.wait_ge(q_stored, 16 * (CREDIT + RBATCH))
            dve.wait_ge(acc_zero, HOPS + 1)

            def edge_sum(i, o):
                g, q = i * CONV_BODY + o, o % GROUPS_IN_BODY
                dve.wait_ge(z_done, g + (CREDIT + 1))
                for j in range(GROUP):
                    dve.wait_ge(gather_done[q * GROUP + j],
                                i * (16 * CONV_BODY // GROUPS_IN_BODY) + 16 * (o // GROUPS_IN_BODY + HOPS * ROUNDS + 1))
                v.tensor_tensor(zs[o % 2], ps_z, gathered[:, q * GROUP:(q + 1) * GROUP, :], ALU.add).then_inc(z_ready, 1)
                dve.wait_ge(z_ready, g + 1)
                dve.sem_inc(slot_free, GROUP)
                dve.sem_inc(z_read, 1)

            def log_sums(g, z):
                dve.wait_ge(logs_ready, g + 1)
                v.scalar_tensor_tensor(out=lg[:, :, 0:FEAT], in0=z[:, :, 0:FEAT], scalar=0.0, in1=lg[:, :, 0:FEAT],
                                       op0=ALU.min, op1=ALU.subtract).then_inc(gate_arg, 1)
                v.scalar_tensor_tensor(out=lg[:, :, FEAT:F2], in0=z[:, :, FEAT:F2], scalar=0.0, in1=lg[:, :, FEAT:F2],
                                       op0=ALU.max, op1=ALU.add).then_inc(soft_ready, 1)

            def messages(g, s):
                dve.wait_ge(gate_ready, g + 1)
                dve.wait_ge(soft_ready, g + 1)
                v.tensor_tensor(msg[:, s, :, 0:FEAT], lg[:, :, 0:FEAT], lg[:, :, FEAT:F2], ALU.mult).then_inc(msg_ready, 1)

            def conv_step(i, o):
                looped = not isinstance(i, int)
                g = i * CONV_BODY + o
                if looped or g:
                    ranks = load_bases(g - 1)
                log_sums(g, zs[o % 2])
                if looped or g + 1 < GROUPS:
                    edge_sum(i, o + 1)
                messages(g, o % 2)
                if looped or g + GROUPS_IN_BODY < GROUPS:
                    next_indices(g * GROUP, o % GROUPS_IN_BODY)

                def ahead(j):
                    if looped or g + 3 < GROUPS:
                        make_pick(g + 3, (o + 3) % GROUPS_IN_BODY, j)

                if looped or g:
                    add_sums(g * GROUP + (HOPS * TILES - GROUP), ranks, FEAT, ps_sums[(o - 1) % 2], ahead)
                else:
                    for j in range(GROUP):
                        ahead(j)

            for g in range(3):
                for j in range(GROUP):
                    make_pick(g, g, j)
            edge_sum(0, 0)
            conv_step(0, 0)
            with dve.Fori(0, CONV_ROUNDS) as i:
                for o in range(1, CONV_BODY + 1):
                    conv_step(i, o)
            for o in TAIL:
                conv_step(CONV_ROUNDS, o)
            add_sums((GROUPS - 1) * GROUP + HOPS * TILES, load_bases(GROUPS - 1), FEAT, ps_sums[(GROUPS - 1) % 2], lambda j: None)

            dve.wait_ge(sums_added, (HOPS + 1) * TILES + CREDIT)

            def add_batch(n, k, s):
                dve.wait_ge(batch_done, n + (CREDIT + 1))
                to = h[:, bass.ds(k * BATCH, BATCH), :]
                v.tensor_tensor(to, to, ps_b[s][:, :, 0:FEAT], ALU.add).then_inc(batch_kept, 1)

            batches(dve, [make_spread, add_batch], HOPS * NBATCH)
            dve.wait_ge(batch_kept, CREDIT + (HOPS + 1) * NBATCH)
            step(v.memset(turned[0][FEAT:FEAT + 1, :, :], 1.0))
            v.memset(turned[1][FEAT:FEAT + 1, :, :], 1.0).then_inc(residual_done, 1)

            def result(n, k, s):
                dve.wait_ge(f_done, n + 1)
                dve.wait_ge(out_stored[s], (n - s) * 8 + 16 * CREDIT)
                v.scalar_tensor_tensor(out=rows_out[s][:, :, 0:FEAT], in0=ps_b[s][:, :, 0:FEAT], scalar=0.0,
                                       in1=xs[:, bass.ds(n * BATCH, BATCH), :],
                                       op0=ALU.max, op1=ALU.add).then_inc(f_kept, 1)

            batches(dve, [result])


def kernel(x, src, dst, edge_attr_32, edge_weight, L1_gnn_Wf, L1_gnn_bf, L1_gnn_Ws, L1_gnn_bs, L1_gnn_Wm, L1_gnn_bm):
    import numpy as np
    import concourse.bacc as bacc
    from concourse.bass_utils import run_bass_kernel_spmd

    def cols(a):
        return np.ascontiguousarray(np.asarray(a).reshape(-1, P).T)

    arrays = {
        "x": np.ascontiguousarray(x),
        "src_t": cols(src),
        "dst_t": cols(dst),
        "dst_rows": np.ascontiguousarray(np.asarray(dst).reshape(-1, P)),
        "w_t": cols(edge_weight),
        "attr_t": np.ascontiguousarray(np.asarray(edge_attr_32).T),
        "w_f": np.ascontiguousarray(L1_gnn_Wf),
        "w_s": np.ascontiguousarray(L1_gnn_Ws),
        "b_f": np.ascontiguousarray(L1_gnn_bf).reshape(1, -1),
        "b_s": np.ascontiguousarray(L1_gnn_bs).reshape(1, -1),
        "w_m": np.ascontiguousarray(L1_gnn_Wm),
        "b_m": np.ascontiguousarray(L1_gnn_bm).reshape(1, -1),
    }
    nc = bacc.Bacc("TRN2", target_bir_lowering=False, num_devices=1)
    args = [nc.dram_tensor(name, a.shape, mybir.dt.from_np(a.dtype), kind="ExternalInput").ap()
            for name, a in arrays.items()]
    out = nc.dram_tensor("out", arrays["x"].shape, F32, kind="ExternalOutput").ap()
    build(nc, *args, out)
    r = run_bass_kernel_spmd(nc, [arrays], core_ids=[0])
    return r.results[0]["out"]
```
